# Optimizing a Trainium2 kernel written in Bass

```python
import numpy as np
import jax
import jax.numpy as jnp

def _softmax(x, axis=-1):
    return jax.nn.softmax(x, axis=axis)
def _gelu(x):
    return jax.nn.gelu(x, approximate=True)
def _silu(x):
    return jax.nn.silu(x)
def _sigmoid(x):
    return jax.nn.sigmoid(x)
def _layernorm(x, axis=-1, eps=1e-5):
    m = jnp.mean(x, axis=axis, keepdims=True)
    v = jnp.var(x, axis=axis, keepdims=True)
    return (x - m) / jnp.sqrt(v + eps)
def _scatter_add(tgt, idx, src, axis=0):
    return tgt.at[idx].add(src)
def _segment_sum(src, seg, n):
    return jax.ops.segment_sum(src, seg, n)

kernel_name = 'mk_adj_resnorm_d4_adj_64_3a7f29'

def setup_inputs(seed: int = 0):
    np.random.seed(seed)
    _w = jnp.asarray
    def _rec_inputs():
        import jax
        import jax.numpy as jnp
        _gk = jax.random.key(seed)
        x = -0.000929 + 1 * jax.random.normal(jax.random.fold_in(_gk, 1), (3327, 64), jnp.float32)
        _a = jax.random.bernoulli(jax.random.fold_in(_gk, 2), 0.00240457, (3327, 3327))
        _a = jnp.logical_or(_a, jnp.swapaxes(_a, -1, -2))
        _a = jnp.logical_or(_a, jnp.eye(3327, dtype=bool))
        _af = _a.astype(jnp.float32)
        _af = _af * jax.random.uniform(jax.random.fold_in(_gk, 3), (3327, 3327), jnp.float32, 0.05, 1)
        adj = _af
        return x, adj
    x, adj = _rec_inputs()
    def _L0_gnn_setup():
        import jax, jax.numpy as jnp
        import numpy as np
        HOP = 2
        N = 16384
        HIDDEN = 64
        key = jax.random.key(seed)
        k1, k2, k3 = jax.random.split(key, 3)
        user_embs = jax.random.normal(k1, (N, HIDDEN), dtype=jnp.float32)
        adj = jax.random.uniform(k2, (N, N), dtype=jnp.float32)
        limit = float(np.sqrt(6.0 / (2 * HIDDEN + HIDDEN)))
        W = jax.random.uniform(k3, (HOP, 2 * HIDDEN, HIDDEN), dtype=jnp.float32, minval=-limit, maxval=limit)
        return {'user_embs': user_embs, 'adj': adj, 'W': W}
    _L0_gnn_all = _L0_gnn_setup()
    _L0_gnn_in = {k: v for k, v in _L0_gnn_all.items() if k in ('W', )}
    del _L0_gnn_all

    def _L1_gnn_setup():
        import jax, jax.numpy as jnp
        import numpy as np
        N = 10000
        DIM = 64
        F_CONST = 1.0
        B_CONST = 0.1
        R_CONST = 0.01
        key = jax.random.key(seed)
        k1, k2 = jax.random.split(key)
        t = jnp.zeros((1,), dtype=jnp.float32)
        x = jax.random.uniform(k1, (N, DIM), dtype=jnp.float32)
        A = jax.random.uniform(k2, (N, N), dtype=jnp.float32)
        return {'t': t, 'x': x, 'A': A}
    _L1_gnn_all = _L1_gnn_setup()
    _L1_gnn_in = {k: v for k, v in _L1_gnn_all.items() if k in ('t', )}
    del _L1_gnn_all

    def _L2_gnn_setup():
        import jax, jax.numpy as jnp
        import numpy as np
        N, D_IN, D_OUT = (8192, 64, 64)
        MAX_NEIGH = 100
        DECAY = 0.5
        key = jax.random.key(seed)
        k1, k2, k3, k4 = jax.random.split(key, 4)
        stdv = 1.0 / np.sqrt(D_OUT)
        inputs = {'input': jax.random.normal(k1, (N, D_IN), dtype=jnp.float32), 'adj': jax.random.randint(k2, (N, N), 0, 2).astype(jnp.float32), 'weight': jax.random.uniform(k3, (D_IN, D_OUT), minval=-stdv, maxval=stdv, dtype=jnp.float32), 'bias': jax.random.uniform(k4, (D_OUT,), minval=-stdv, maxval=stdv, dtype=jnp.float32)}
        return inputs
    _L2_gnn_all = _L2_gnn_setup()
    _L2_gnn_in = {k: v for k, v in _L2_gnn_all.items() if k in ('weight', 'bias', )}
    del _L2_gnn_all

    def _L3_gnn_setup():
        import jax, jax.numpy as jnp
        import numpy as np
        N = 4096
        D = 64
        NUM_LAYERS = 2
        THETA0 = 0.000244
        THETA_MAX = 0.0003
        LAM = 0.1
        TAU = 1.0
        EPS = 1e-06
        H_DENSITY = 0.005

        def _safe_norm(x, axis):
            return jnp.sqrt(jnp.maximum(jnp.sum(x * x, axis=axis), 1e-16))

        def _layer(x, H, W, Theta, Wq, bq, Wv, bv, iteration):
            scale = D ** (-0.5)
            theta_base = THETA0 + (1.0 - np.exp(-LAM * iteration)) * (THETA_MAX - THETA0)
            th_comp = theta_base
            th_edge = min(theta_base, 0.8)
            th_node = min(theta_base, 0.7)
            structural = _safe_norm(x @ W, axis=1)
            Q = x @ Wq + bq
            V = x @ Wv + bv
            edge_feat = H.T @ V
            att = Q @ edge_feat.T * scale * H
            att = jax.nn.softmax(att, axis=1)
            att_scores = att.mean(axis=0)
            importance = 0.5 * structural + 0.5 * att_scores
            comp_scores = jax.nn.softmax(importance / TAU)
            comp_mask = comp_scores >= th_comp
            x_comp = x * comp_mask[:, None]
            nrm = jnp.maximum(_safe_norm(x_comp, axis=1), 1e-08)
            xn = x_comp / nrm[:, None]
            cos = xn @ xn.T
            edge_scores = jax.nn.softmax(cos * H / TAU, axis=1)
            edge_mask = (edge_scores >= th_edge) & comp_mask[:, None]
            H_pruned = H * edge_mask
            connectivity = H_pruned.sum(axis=1)
            feat_mag = _safe_norm(x_comp, axis=1)
            node_scores = jax.nn.softmax(connectivity * feat_mag / TAU)
            connected = (H_pruned * edge_mask).sum(axis=1) > 0
            node_mask = (node_scores >= th_node) & connected
            x_final = x_comp * node_mask[:, None]
            vdeg = jnp.maximum(H_pruned.sum(axis=1), EPS)
            edeg = jnp.maximum(H_pruned.sum(axis=0), EPS)
            dv_isqrt = 1.0 / jnp.sqrt(vdeg)
            de_inv = 1.0 / edeg
            transformed = x_final @ W
            agg = H_pruned.T * dv_isqrt[None, :] @ transformed
            agg = agg * de_inv[:, None]
            msg = dv_isqrt[:, None] * (H_pruned @ agg)
            msg = msg @ Theta
            return jax.nn.relu(msg)
        key = jax.random.key(seed)
        ks = jax.random.split(key, 8)
        xav = 0.125
        X = jax.random.normal(ks[0], (N, D), jnp.float32) * 0.05
        W = jax.random.normal(ks[1], (D, D), jnp.float32) * xav
        Theta = jax.random.normal(ks[2], (D, D), jnp.float32) * xav
        Wq = jax.random.normal(ks[3], (D, D), jnp.float32) * xav
        bq = jnp.zeros((D,), jnp.float32)
        Wv = jax.random.normal(ks[4], (D, D), jnp.float32) * xav
        bv = jnp.zeros((D,), jnp.float32)
        H = (jax.random.uniform(ks[7], (N, N)) < H_DENSITY).astype(jnp.float32)
        return {'X': X, 'W': W, 'Theta': Theta, 'Wq': Wq, 'bq': bq, 'Wv': Wv, 'bv': bv, 'H': H}
    _L3_gnn_all = _L3_gnn_setup()
    _L3_gnn_in = {k: v for k, v in _L3_gnn_all.items() if k in ('W', 'Theta', 'Wq', 'bq', 'Wv', 'bv', )}
    del _L3_gnn_all

    return {
        "x": x,
        "adj": adj,
        "L0_gnn_W": _L0_gnn_in["W"],
        "L1_gnn_t": _L1_gnn_in["t"],
        "L2_gnn_weight": _L2_gnn_in["weight"],
        "L2_gnn_bias": _L2_gnn_in["bias"],
        "L3_gnn_W": _L3_gnn_in["W"],
        "L3_gnn_Theta": _L3_gnn_in["Theta"],
        "L3_gnn_Wq": _L3_gnn_in["Wq"],
        "L3_gnn_bq": _L3_gnn_in["bq"],
        "L3_gnn_Wv": _L3_gnn_in["Wv"],
        "L3_gnn_bv": _L3_gnn_in["bv"],
    }

def reference(x, adj, L0_gnn_W, L1_gnn_t, L2_gnn_weight, L2_gnn_bias, L3_gnn_W, L3_gnn_Theta, L3_gnn_Wq, L3_gnn_bq, L3_gnn_Wv, L3_gnn_bv):
    import jax
    import jax.numpy as jnp
    def _L0_gnn_ref(user_embs, adj, W):
        import jax, jax.numpy as jnp
        import numpy as np
        HOP = 2
        N = 16384
        HIDDEN = 64
        x = user_embs
        for k in range(HOP):
            agg = adj @ x
            x = jnp.tanh(jnp.concatenate([agg, x], axis=1) @ W[k])
        return x

    def _L1_gnn_ref(t, x, A):
        import jax, jax.numpy as jnp
        import numpy as np
        N = 10000
        DIM = 64
        F_CONST = 1.0
        B_CONST = 0.1
        R_CONST = 0.01
        Ax = A @ x
        outer = R_CONST * jnp.sum(x * Ax, axis=1, keepdims=True)
        return F_CONST - B_CONST * x - outer

    def _L2_gnn_ref(input, adj, weight, bias):
        import jax, jax.numpy as jnp
        import numpy as np
        N, D_IN, D_OUT = (8192, 64, 64)
        MAX_NEIGH = 100
        DECAY = 0.5
        support = input @ weight
        mask = (adj != 0).astype(support.dtype)
        rank = jnp.cumsum(mask, axis=1)
        deg = rank[:, -1:]
        k = jnp.minimum(deg, float(MAX_NEIGH))
        pos = rank - (deg - k)
        w = mask * jnp.where(pos > 0, DECAY ** (k - pos), 0.0)
        out = w @ support + bias
        return out

    def _L3_gnn_ref(X, W, Theta, Wq, bq, Wv, bv, H):
        import jax, jax.numpy as jnp
        import numpy as np
        N = 4096
        D = 64
        NUM_LAYERS = 2
        THETA0 = 0.000244
        THETA_MAX = 0.0003
        LAM = 0.1
        TAU = 1.0
        EPS = 1e-06
        H_DENSITY = 0.005

        def _safe_norm(x, axis):
            return jnp.sqrt(jnp.maximum(jnp.sum(x * x, axis=axis), 1e-16))

        def _layer(x, H, W, Theta, Wq, bq, Wv, bv, iteration):
            scale = D ** (-0.5)
            theta_base = THETA0 + (1.0 - np.exp(-LAM * iteration)) * (THETA_MAX - THETA0)
            th_comp = theta_base
            th_edge = min(theta_base, 0.8)
            th_node = min(theta_base, 0.7)
            structural = _safe_norm(x @ W, axis=1)
            Q = x @ Wq + bq
            V = x @ Wv + bv
            edge_feat = H.T @ V
            att = Q @ edge_feat.T * scale * H
            att = jax.nn.softmax(att, axis=1)
            att_scores = att.mean(axis=0)
            importance = 0.5 * structural + 0.5 * att_scores
            comp_scores = jax.nn.softmax(importance / TAU)
            comp_mask = comp_scores >= th_comp
            x_comp = x * comp_mask[:, None]
            nrm = jnp.maximum(_safe_norm(x_comp, axis=1), 1e-08)
            xn = x_comp / nrm[:, None]
            cos = xn @ xn.T
            edge_scores = jax.nn.softmax(cos * H / TAU, axis=1)
            edge_mask = (edge_scores >= th_edge) & comp_mask[:, None]
            H_pruned = H * edge_mask
            connectivity = H_pruned.sum(axis=1)
            feat_mag = _safe_norm(x_comp, axis=1)
            node_scores = jax.nn.softmax(connectivity * feat_mag / TAU)
            connected = (H_pruned * edge_mask).sum(axis=1) > 0
            node_mask = (node_scores >= th_node) & connected
            x_final = x_comp * node_mask[:, None]
            vdeg = jnp.maximum(H_pruned.sum(axis=1), EPS)
            edeg = jnp.maximum(H_pruned.sum(axis=0), EPS)
            dv_isqrt = 1.0 / jnp.sqrt(vdeg)
            de_inv = 1.0 / edeg
            transformed = x_final @ W
            agg = H_pruned.T * dv_isqrt[None, :] @ transformed
            agg = agg * de_inv[:, None]
            msg = dv_isqrt[:, None] * (H_pruned @ agg)
            msg = msg @ Theta
            return jax.nn.relu(msg)
        x = X
        for it in range(NUM_LAYERS):
            x = _layer(x, H, W, Theta, Wq, bq, Wv, bv, it)
        return x

    x = _layernorm(x + _L0_gnn_ref(x, adj, L0_gnn_W), axis=-1)
    x = _layernorm(x + _L1_gnn_ref(L1_gnn_t, x, adj), axis=-1)
    x = _layernorm(x + _L2_gnn_ref(x, adj, L2_gnn_weight, L2_gnn_bias), axis=-1)
    x = _layernorm(x + _L3_gnn_ref(x, L3_gnn_W, L3_gnn_Theta, L3_gnn_Wq, L3_gnn_bq, L3_gnn_Wv, L3_gnn_bv, adj), axis=-1)
    return x


_drawn_inputs = setup_inputs


def setup_inputs(seed=0):
    import zlib

    import numpy as np

    out = dict(_drawn_inputs(seed))
    spreads = {'L3_gnn_bq': (0.0, 0.1), 'L3_gnn_bv': (0.0, 0.1)}
    factors = {'L3_gnn_W': 8.0, 'L3_gnn_Theta': 8.0}
    for name, (base, spread) in spreads.items():
        noise = np.random.default_rng([zlib.crc32(name.encode()), seed]).standard_normal(out[name].shape)
        drawn = base * np.exp(spread * noise) if base else spread * noise
        out[name] = jnp.asarray(drawn.astype(out[name].dtype))
    for name, factor in factors.items():
        out[name] = (out[name] * factor).astype(out[name].dtype)
    return out
```

```python
from contextlib import ExitStack

import concourse.bass as bass
import numpy as np
from concourse import mybir

F32 = mybir.dt.float32
BF16 = mybir.dt.bfloat16
I16 = mybir.dt.int16
I8 = mybir.dt.int8
ALU = mybir.AluOpType
ACT = mybir.ActivationFunctionType
X = mybir.AxisListType.X
RMAX = bass.bass_isa.ReduceOp.max
RADD = bass.bass_isa.ReduceOp.add

N = 3327
D = 64
P = 128
NB = (N + P - 1) // P
NP = NB * P
HALF = NP // 2
HB = NB // 2
RING = 4
BANK = 512
HALF_CHUNKS = [(o, min(BANK, HALF - o)) for o in range(0, HALF, BANK)]
QUART = HALF // 2
QUART_CHUNKS = [(o, min(BANK, QUART - o)) for o in range(0, QUART, BANK)]
PIECE = 9 * P
PIECES = [(o, min(PIECE, NP - o)) for o in range(0, NP, PIECE)]
ROW_CHUNKS = [(o, min(BANK, NP - o)) for o in range(0, NP, BANK)]
LN_EPS = 1e-5
HUGE = 1e30
NEIGHBOURS = 100
DECAY_SHIFT = 27
MARK = 1 << 14
THETA0, THETA_MAX, LAM = 0.000244, 0.0003, 0.1
WEIGHTS = ["w0_agg", "w0_self", "w1_agg", "w1_self", "decay_w", "hyper_w", "theta", "value_w", "query_w", "query_w2"]

PASSES = [("hop0", NB), ("hop1", NB), ("ode", NB), ("decay0", NB), ("decay1", NB)]
for _it in range(2):
    PASSES += [(f"{s}{_it}", NB) for s in ("edge", "att", "cos", "down", "up")]
BASE = {}
_n = 0
for _name, _count in PASSES:
    BASE[_name] = _n
    _n += _count
AGGS = ["hop0", "hop1", "ode", "decay", "edge0", "down0", "up0", "edge1", "down1", "up1"]
PRODUCTS = ["att0", "cos0", "att1", "cos1"]


def thresholds(it):
    base = THETA0 + (1.0 - np.exp(-LAM * it)) * (THETA_MAX - THETA0)
    return float(base), float(min(base, 0.8)), float(min(base, 0.7))


def build_program(nc, adj, adj_t, x_nodes, x_feat, weights, rows, bq, consts, decay_consts, x_kept, out):
    ctx = ExitStack()
    with ctx:
        def sb(name, cols, dt):
            return ctx.enter_context(nc.sbuf_tensor(name, [P, cols], dt))

        def sem(name):
            return ctx.enter_context(nc.semaphore(name))

        slots = [sb(f"slot{i}", NP, F32) for i in range(RING)]
        arena = sb("arena", NB * NP // 4, F32)
        signs = arena[:, :].bitcast(I8)
        signs3 = signs.rearrange("p (b n) -> p b n", b=NB)
        pairs = sb("pairs", 2 * NP, F32)
        prod = [pairs[:, i * NP:(i + 1) * NP] for i in range(2)]
        agg_f = pairs[:, 0:HALF]
        col_rows = pairs[:, HALF:HALF + 2 * BANK]
        xw = sb("xw", NB * D, F32)
        cur = sb("cur", NB * D, F32)
        right12 = sb("right12", NP, BF16)
        right21 = sb("right21", NP, BF16)
        right31 = sb("right31", NP, BF16)
        cos13 = cur[:, :].bitcast(BF16)

        off = [0]

        def work(words):
            a = arena[:, off[0]:off[0] + words]
            off[0] += words
            return a
        xt = work(HALF)
        scr_a = work(NB * D)
        scr_b = work(NB * D)
        full = work(NP)
        rest = work(NP)
        part1 = work(NP // 2).bitcast(BF16)
        part2 = work(NP // 2).bitcast(BF16)
        part3 = work(NP // 2).bitcast(BF16)
        query12 = work(NP // 2).bitcast(BF16)
        query13 = work(NP // 2).bitcast(BF16)
        assert off[0] <= NB * NP // 4
        support3 = full.bitcast(BF16)[:, 0:NB * 3 * D]
        nbr = [pairs[:, HALF + i * QUART:HALF + (i + 1) * QUART].bitcast(BF16) for i in range(2)]
        decay = [pairs[:, HALF + (2 + i) * QUART:HALF + (3 + i) * QUART] for i in range(2)]
        tri = right31[:, 0:P]
        rest_tri = right31[:, P:2 * P]
        start_bits = right31[:, 2 * P:3 * P]
        stat3 = [right31[:, (3 + 2 * i) * P:(3 + 2 * i) * P + 3 * D] for i in range(2)]
        sign_cols = [right12[:, :], right21[:, :]]

        wt = sb("wt", len(WEIGHTS) * D, F32)
        W = {n: wt[:, i * D:(i + 1) * D] for i, n in enumerate(WEIGHTS)}
        rowt = sb("rowt", 2 * D + 1, F32)
        decay_bias, value_bias, query_bias = rowt[:, 0:D], rowt[:, D:2 * D], rowt[:, 2 * D:2 * D + 1]
        cst = sb("cst", 2 * P + 2 * NB, F32)
        ident, twice = cst[:, 0:P], cst[:, P:2 * P]
        real, not_real = cst[:, 2 * P:2 * P + NB], cst[:, 2 * P + NB:2 * P + 2 * NB]
        ident_b = sb("ident_b", P, BF16)
        zeros_b = sb("zeros_b", P, BF16)
        ones_b = sb("ones_b", BANK, BF16)
        ones32 = sb("ones32", 32, F32)
        stat = sb("stat", 2 * D, F32)
        rz32 = sb("rz32", 2 * 32, F32)
        small = {n: sb(n, NB, F32) for n in
                 ("mean", "var", "structural", "colsum", "imp", "comp", "blocked", "norm", "rnorm",
                  "conn", "node_z", "node_e", "dv", "edeg")}
        tiny = {n: sb(n, 1, F32) for n in ("pmax", "gmax", "ngmax", "psum_", "gsum", "thr", "query_shift")}
        max3 = sb("max3", 2 * 3, F32)
        rowmax = sb("rowmax", 2, F32)
        gates = sb("gates", 6, F32)
        negmax = sb("negmax", 2, F32)
        rowsum = sb("rowsum", 2, F32)
        cut = sb("cut", 2, F32)
        negcut = sb("negcut", 2, F32)
        eps_t = sb("eps_t", 1, F32)

        ps = ctx.enter_context(nc.psum_tensor("ps", [P, 8 * BANK], F32))

        def bank(b, cols=BANK, at=0):
            return ps[:, b * BANK + at:b * BANK + at + cols]

        def by_half(t):
            return t.rearrange("p (h b d) -> p h b d", h=2, d=D)

        def node_psum(first):
            v = ps[:, first * BANK:(first + 4) * BANK].rearrange("p (h n) -> p h n", h=2)
            return v[:, :, 0:HB * D].rearrange("p h (b d) -> p h b d", d=D)

        def per_node(t):
            return t.unsqueeze(2).to_broadcast([P, NB, D])

        def per_node4(t):
            return t.rearrange("p (h b) -> p h b", h=2).unsqueeze(3).to_broadcast([P, 2, HB, D])

        def per_feature4(t):
            return t.unsqueeze(1).unsqueeze(1).to_broadcast([P, 2, HB, D])

        def blocks3(t):
            return t.rearrange("p (b d) -> p b d", d=D)

        slot_loaded = [sem(f"slot_loaded{i}") for i in range(RING)]
        block_done = sem("block_done")
        stat_ready = sem("stat_ready")
        const_loaded = sem("const_loaded")
        consts_made = sem("consts_made")
        consts_cast = sem("consts_cast")
        evac_act = sem("evac_act")
        evac_dve = sem("evac_dve")
        folded = sem("folded")
        x_ready = sem("x_ready")
        xt_psum = sem("xt_psum")
        xt_act = sem("xt_act")
        xt_dve = sem("xt_dve")
        dve_chain = sem("dve_chain")
        ln_var = sem("ln_var")
        ln_sd = sem("ln_sd")
        tanh_done = sem("tanh_done")
        support_psum = sem("support_psum")
        support_ready = sem("support_ready")
        tri_done = sem("tri_done")
        relu_act = sem("relu_act")
        relu_dve = sem("relu_dve")
        decay_used = sem("decay_used")
        kept = sem("kept")
        kept_read = sem("kept_read")
        proj_psum = sem("proj_psum")
        proj_read = sem("proj_read")
        struct_sq = sem("struct_sq")
        struct_done = sem("struct_done")
        query_f32 = sem("query_f32")
        parts = sem("parts")
        cut_act = sem("cut_act")
        cut_ready = sem("cut_ready")
        half_done = sem("half_done")
        dup_psum = sem("dup_psum")
        piece_ready = sem("piece_ready")
        piece_read = sem("piece_read")
        rowmax_done = sem("rowmax_done")
        negmax_ready = sem("negmax_ready")
        exp_done = sem("exp_done")
        rz_done = sem("rz_done")
        rz_ready = sem("rz_ready")
        cut_done = sem("cut_done")
        negcut_ready = sem("negcut_ready")
        pruned = sem("pruned")
        product_free = sem("product_free")
        colsum_psum = sem("colsum_psum")
        colsum_sbuf = sem("colsum_sbuf")
        colsum_t = sem("colsum_t")
        part_max = sem("part_max")
        all_max = sem("all_max")
        part_sum = sem("part_sum")
        all_sum = sem("all_sum")
        soft_bias = sem("soft_bias")
        norm_sq = sem("norm_sq")
        norm_rt = sem("norm_rt")
        normed = sem("normed")
        deg_sq = sem("deg_sq")
        deg_rt = sem("deg_rt")
        down_ready = sem("down_ready")
        up_ready = sem("up_ready")
        value_ready = sem("value_ready")
        col_ready = sem("col_ready")
        signs_t = sem("signs_t")
        up_pruned = sem("up_pruned")
        out_ready = sem("out_ready")
        stored = sem("stored")

        block = ctx.enter_context(nc.Block())

        def each_block(eng, body):
            head = NB % RING
            for k in range(head):
                body(k, 0)
            with eng.Fori(0, NB // RING) as i:
                for k in range(head, head + RING):
                    body(k, i)

        def landed(eng, name, k, i):
            n = BASE[name] + k
            eng.wait_ge(slot_loaded[n % RING], (n // RING + i + 1) * 16)
            return slots[n % RING]

        def slot_of(name, k):
            return slots[(BASE[name] + k) % RING]

        @block.sync
        def _(sp):
            sp.dma_start(xw[:, :], x_nodes).then_inc(const_loaded, 16)
            sp.dma_start(xt, x_feat).then_inc(const_loaded, 16)
            sp.dma_start(cst[:, :], consts).then_inc(const_loaded, 16)
            sp.dma_start(wt[:, :], weights).then_inc(const_loaded, 16)
            sp.dma_start(rowt[:, 0:2 * D], rows).then_inc(const_loaded, 16)
            sp.dma_start(rowt[:, 2 * D:2 * D + 1], bq).then_inc(const_loaded, 16)
            sp.dma_start(rest[:, 0:2 * P], decay_consts).then_inc(const_loaded, 16)

            def stream(name, source, quarter=None):
                def load(k, i):
                    n = BASE[name] + k
                    row = i * (RING * P) + k * P if quarter is None else i * (-RING * P) + (NB - 1 - k) * P
                    row = row if isinstance(row, int) else sp.snap(row)
                    sp.wait_ge(block_done, i * RING + (n + 1))
                    slot = slots[n % RING]
                    if quarter is None:
                        src, dst = source[bass.ds(row, P), :], slot[:, :]
                    else:
                        src = source[bass.ds(row, P), :].rearrange("p (h n) -> p h n", h=2)
                        src = src[:, :, quarter * QUART:(quarter + 1) * QUART]
                        dst = slot[:, 0:2 * QUART].rearrange("p (h n) -> p h n", h=2)
                    sp.dma_start(dst, src).then_inc(slot_loaded[n % RING], 16)
                each_block(sp, load)

            stream("hop0", adj_t)
            stream("hop1", adj_t)
            stream("ode", adj_t)
            stream("decay0", adj_t, 0)
            stream("decay1", adj_t, 1)
            for it in range(2):
                if it == 0:
                    sp.wait_ge(x_ready, 4)
                    sp.dma_start(x_kept, cur[:, :]).then_inc(kept, 16)
                stream(f"edge{it}", adj)
                if it == 0:
                    sp.wait_ge(kept, 16)
                    sp.sem_inc(kept_read, 1)
                stream(f"att{it}", adj)
                stream(f"cos{it}", adj)
                stream(f"down{it}", adj)
                if it == 1:
                    sp.wait_ge(down_ready, 2)
                    sp.dma_start(xw[:, :], x_kept).then_inc(kept, 16)
                stream(f"up{it}", adj_t)
            sp.wait_ge(out_ready, 1)
            sp.dma_start(out, blocks3(cur[:, :])[:, :, :]).then_inc(stored, 16)
            sp.wait_ge(stored, 16)

        @block.gpsimd
        def _(pool):
            pool.memset(zeros_b[:, :], 0.0).then_inc(consts_made, 1)
            pool.memset(ones_b[:, :], 1.0).then_inc(consts_made, 1)
            pool.memset(ones32[:, :], 1.0).then_inc(consts_made, 1)
            pool.memset(start_bits, -float(MARK - NEIGHBOURS * P) / P).then_inc(consts_made, 1)
            pool.memset(eps_t[:, :], LN_EPS).then_inc(consts_made, 1)

            def feed(name, source):
                def copy(k, i):
                    pool.wait_ge(block_done, i * RING + (BASE[name] + k + RING - 1))
                    pool.tensor_copy(stat[:, k % 2 * D:(k % 2 + 1) * D],
                                     source[:, bass.ds(i * (RING * D) + k * D, D)]).then_inc(stat_ready, 1)
                each_block(pool, copy)

            def feed_decay(q):
                def copy(k, i):
                    pool.wait_ge(decay_used, i * RING + (q * NB + k + 1))
                    pool.tensor_copy(stat3[k % 2], support3[:, bass.ds(i * (-RING * 3 * D) + (NB - 1 - k) * 3 * D, 3 * D)])\
                        .then_inc(stat_ready, 1)
                each_block(pool, copy)

            def node_softmax(r):
                pool.wait_ge(part_max, r + 1)
                pool.partition_all_reduce(tiny["gmax"][:, :], tiny["pmax"][:, :], P, RMAX).then_inc(all_max, 1)
                pool.wait_ge(part_sum, r + 1)
                pool.partition_all_reduce(tiny["gsum"][:, :], tiny["psum_"][:, :], P, RADD).then_inc(all_sum, 1)

            pool.wait_ge(const_loaded, 7 * 16)
            feed("hop0", xw)
            pool.wait_ge(x_ready, 1)
            feed("hop1", cur)
            pool.wait_ge(x_ready, 2)
            feed("ode", cur)
            pool.wait_ge(support_ready, 1)
            feed_decay(0)
            feed_decay(1)
            for it in range(2):
                pool.wait_ge(value_ready, it + 1)
                feed(f"edge{it}", scr_a)
                node_softmax(2 * it)
                node_softmax(2 * it + 1)
                pool.wait_ge(down_ready, it + 1)
                feed(f"down{it}", cur)
                pool.wait_ge(up_ready, it + 1)
                feed(f"up{it}", cur)

        @block.tensor
        def _(pe):
            pe.sem_inc(block_done, RING)
            pe.sem_inc(piece_read, 2)
            pe.sem_inc(product_free, 2)
            pe.sem_inc(decay_used, 2)
            pe.sem_inc(signs_t, 8)
            pe.sem_inc(up_pruned, 2)
            pe.wait_ge(const_loaded, 7 * 16)
            pe.wait_ge(consts_made, 5)
            pe.wait_ge(consts_cast, 3)

            stats_before = {n: sum(2 * NB if a == "decay" else NB for a in AGGS[:AGGS.index(n)]) for n in AGGS}

            halves = [0]

            def mm(o, l, r, start=True, stop=True):
                return pe.matmul(o, l, r, start=start, stop=stop, skip_group_check=True)

            def aggregate(name, pruned_base=None):
                def step(k, i):
                    if pruned_base is None:
                        slot = landed(pe, name, k, i)
                    else:
                        slot = slot_of(name, k)
                        pe.wait_ge(pruned, i * RING + (pruned_base + k + 1))
                    pe.wait_ge(stat_ready, i * RING + (stats_before[name] + k + 1))
                    s = stat[:, k % 2 * D:(k % 2 + 1) * D]
                    for o, w in HALF_CHUNKS:
                        for h in range(2):
                            last = mm(ps[h * D:(h + 1) * D, o:o + w], s, slot[:, h * HALF + o:h * HALF + o + w],
                                      start=k == 0)
                    last.then_inc(block_done, 1)
                each_block(pe, step)

            def fold(e, right, first=4, also=None):
                pe.wait_ge(evac_act, e + 1)
                pe.wait_ge(evac_dve, e + 1)
                return to_nodes(agg_f, right, first, also)

            def to_nodes(left, right, first, also=None):
                for b in range(HB):
                    for h in range(2):
                        o = bank(first + 2 * h, at=b * D, cols=D)
                        last = mm(o, left[h * D:(h + 1) * D, b * P:(b + 1) * P], right[h * D:(h + 1) * D, :])
                        if also is not None:
                            last = mm(o, xt[h * D:(h + 1) * D, b * P:(b + 1) * P], also[h * D:(h + 1) * D, :],
                                      start=False)
                return last

            def to_features(source, first):
                for b in range(HB):
                    for h in range(2):
                        last = mm(ps[h * D:(h + 1) * D, first * BANK + b * P:first * BANK + (b + 1) * P],
                                  source[:, (h * HB + b) * D:(h * HB + b + 1) * D], ident)
                return last

            def on_both_halves(left, right):
                edges = sorted({o for o, _ in ROW_CHUNKS} | {HALF, NP})
                halves[0] += 1
                for o, e in zip(edges, edges[1:]):
                    h = o // HALF
                    last = mm(ps[:, o:e], left[h * D:(h + 1) * D, :], right[h * D:(h + 1) * D, o - h * HALF:e - h * HALF])
                    if e == HALF:
                        last.then_inc(half_done, 1)
                        pe.wait_ge(half_done, halves[0])
                return last

            def features_round(r):
                pe.wait_ge(x_ready, r)
                to_features(cur[:, :], 0).then_inc(xt_psum, 1)

            aggregate("hop0")
            fold(0, W["w0_agg"], also=W["w0_self"]).then_inc(folded, 1)
            features_round(1)
            pe.wait_ge(xt_act, 1)
            pe.wait_ge(xt_dve, 1)
            aggregate("hop1")
            fold(1, W["w1_agg"], also=W["w1_self"]).then_inc(folded, 1)
            aggregate("ode")
            fold(2, twice[:, 0:D]).then_inc(folded, 1)
            features_round(3)
            pe.wait_ge(xt_act, 2)
            pe.wait_ge(xt_dve, 2)
            to_nodes(xt, W["decay_w"], 4).then_inc(support_psum, 1)
            pe.wait_ge(support_ready, 1)

            for q in range(2):
                if q:
                    pe.wait_ge(relu_act, 2 * NB)
                    pe.wait_ge(relu_dve, 2 * NB)
                for b in range(4):
                    mm(bank(b), start_bits, ones_b[:, :])

                def step(k, i, q=q):
                    n = BASE[f"decay{q}"] + k
                    pe.wait_ge(block_done, i * RING + (n + 1 + RING))
                    pe.wait_ge(stat_ready, i * RING + (stats_before["decay"] + q * NB + k + 1))
                    nb = nbr[k % 2]
                    for o, w in QUART_CHUNKS:
                        for s in range(2):
                            b = 2 * s + o // BANK
                            mm(bank(b, w), tri, nb[:, s * QUART + o:s * QUART + o + w], start=False)\
                                .then_inc(tri_done, 1)
                    for c, (o, w) in enumerate(QUART_CHUNKS):
                        pe.wait_ge(relu_act, i * (2 * RING) + (2 * (q * NB + k) + c + 1))
                        pe.wait_ge(relu_dve, i * (2 * RING) + (2 * (q * NB + k) + c + 1))
                        for s in range(2):
                            mm(bank(2 * s + c, w), rest_tri, nb[:, s * QUART + o:s * QUART + o + w], start=False)
                        dw = decay[k % 2].bitcast(BF16)
                        for part in range(3):
                            for s in range(2):
                                last = mm(ps[s * D:(s + 1) * D, (4 + 2 * q + c) * BANK:(4 + 2 * q + c) * BANK + w],
                                          stat3[k % 2][:, part * D:(part + 1) * D],
                                          dw[:, s * QUART + o:s * QUART + o + w], start=k == 0 and part == 0)
                    last.then_inc(decay_used, 1)
                each_block(pe, step)
            fold(3, twice[:, 0:D], first=0).then_inc(folded, 1)

            def product(name, left12, left13):
                g = PRODUCTS.index(name)
                sums = name.startswith("att")
                for b in (6, 7):
                    mm(bank(b), zeros_b[:, :], ones_b[:, :])

                def pieces(k, i):
                    at = i * (RING * P) + k * P
                    for c, (o, w) in enumerate(PIECES):
                        buf = (k + c) % 2
                        pe.wait_ge(piece_read, i * (RING * 3) + ((g * NB + k) * 3 + c + 1))
                        for n, (left, right) in enumerate(((left12, right12), (left12, right21), (left13, right31))):
                            for s in range(0, w, BANK):
                                v = min(BANK, w - s)
                                last = mm(bank(3 * buf, v, s), left[:, bass.ds(at, P)], right[:, o + s:o + s + v],
                                          start=n == 0)
                        last.then_inc(piece_ready, 1)

                def columns(k, i):
                    if sums:
                        pe.wait_ge(rz_ready, i * RING + (g // 2 * NB + k + 1))
                        moving, s = prod[k % 2], rz32[:, k % 2 * 32:(k % 2 + 1) * 32]
                    else:
                        pe.wait_ge(pruned, i * RING + (g // 2 * 2 * NB + k + 1))
                        moving, s = slot_of(name, k), ones32[:, :]
                    for c, (o, w) in enumerate(ROW_CHUNKS):
                        r = c % 4
                        w = min(w, N - o)
                        last = mm(ps[32 * r:32 * r + 32, (6 + c // 4) * BANK:(6 + c // 4) * BANK + w], s,
                                  moving[:, o:o + w], start=False)
                    last.then_inc(product_free if sums else block_done, 1)
                    return last

                pieces(0, 0)
                pieces(1, 0)
                columns(0, 0)
                with pe.Fori(0, NB // RING) as i:
                    for k in range(2, 2 + RING):
                        pieces(k, i)
                        columns(k - 1, i)
                columns(NB % RING - 1 + RING, NB // RING - 1)
                mm(bank(0, 1), zeros_b[:, :], ones_b[:, 0:1]).then_inc(colsum_psum, 1)
                pe.wait_ge(colsum_sbuf, g + 1)
                for t in range(8):
                    last = pe.transpose(ps[:, t * P:(t + 1) * P], col_rows[:, t * P:(t + 1) * P], ident)
                last.then_inc(colsum_t, 1)

            for it in range(2):
                features_round(4 + it)
                pe.wait_ge(xt_act, 3 + it)
                pe.wait_ge(xt_dve, 3 + it)
                to_nodes(xt, W["hyper_w"], 4).then_inc(proj_psum, 1)
                to_nodes(xt, W["value_w"], 0).then_inc(proj_psum, 1)
                pe.wait_ge(proj_read, it + 1)
                pe.wait_ge(value_ready, it + 1)
                query = wt[:, WEIGHTS.index("query_w") * D:(WEIGHTS.index("query_w") + 2) * D]
                on_both_halves(query, xt).then_inc(dup_psum, 1)
                pe.wait_ge(query_f32, it + 1)
                aggregate(f"edge{it}")
                pe.wait_ge(evac_act, 5 + 3 * it)
                pe.wait_ge(evac_dve, 5 + 3 * it)
                on_both_halves(twice, agg_f).then_inc(dup_psum, 1)
                pe.wait_ge(cut_ready, 3 * it + 2)
                product(f"att{it}", query12, query13)
                pe.wait_ge(normed, it + 1)
                for b in range(NB):
                    for h in range(2):
                        last = mm(ps[h * D:(h + 1) * D, b * P:(b + 1) * P], scr_a[:, b * D:(b + 1) * D], ident)
                last.then_inc(dup_psum, 1)
                pe.wait_ge(cut_ready, 3 * it + 3)
                product(f"cos{it}", right12, cos13)
                aggregate(f"down{it}", pruned_base=(2 * it + 1) * NB)
                fold(5 + 3 * it, twice[:, 0:D]).then_inc(folded, 1)

                name = f"up{it}"
                pe.wait_ge(up_ready, it + 1)

                def turn(k, i, c, it=it):
                    o, w = HALF_CHUNKS[c]
                    if c == 0:
                        pe.wait_ge(col_ready, i * RING + (it * NB + k + 1))
                    pe.wait_ge(up_pruned, i * (4 * RING) + (4 * (it * NB + k) + c + 1))
                    for h in range(2):
                        for t in range(0, w, P):
                            last = mm(bank(4 + 2 * (c % 2) + h, P, t),
                                      sign_cols[k % 2][:, h * HALF + o + t:h * HALF + o + t + P], ident_b[:, :])
                    last.then_inc(signs_t, 1)

                def gather(k, i, c, it=it, name=name):
                    o, w = HALF_CHUNKS[c]
                    slot = slot_of(name, k)
                    pe.wait_ge(up_pruned, i * (4 * RING) + (4 * (it * NB + k) + c + 3))
                    if c == 0:
                        pe.wait_ge(stat_ready, i * RING + (stats_before[name] + k + 1))
                    for h in range(2):
                        last = mm(ps[h * D:(h + 1) * D, o:o + w], stat[:, k % 2 * D:(k % 2 + 1) * D],
                                  slot[:, h * HALF + o:h * HALF + o + w], start=k == 0)
                    if c == 3:
                        last.then_inc(block_done, 1)

                def up_step(k, i):
                    turn(k, i, 0)
                    if k > 0:
                        gather(k - 1, i, 3)
                    for c in range(1, 4):
                        turn(k, i, c)
                        gather(k, i, c - 1)
                each_block(pe, up_step)
                gather(NB % RING - 1 + RING, NB // RING - 1, 3)
                fold(6 + 3 * it, W["theta"]).then_inc(folded, 1)

        @block.scalar
        def _(act):
            def evac(n_done, e):
                act.wait_ge(block_done, RING + n_done)
                act.activation(agg_f[:, 0:2 * BANK], ps[:, 0:2 * BANK], ACT.Copy).then_inc(evac_act, 1)

            def features(r):
                act.wait_ge(xt_psum, r + 1)
                act.activation(xt[:, 0:2 * BANK], ps[:, 0:2 * BANK], ACT.Copy).then_inc(xt_act, 1)

            def root(dst, src, ready, n, done, bias=0.0):
                act.wait_ge(ready, n)
                act.activation(dst, src, ACT.Sqrt, bias=bias).then_inc(done, 1)

            lns = [0]

            def layernorm_root():
                lns[0] += 1
                root(small["var"][:, :], small["mean"][:, :], ln_var, lns[0], ln_sd, bias=eps_t[:, 0:1])

            act.wait_ge(consts_made, 5)
            evac(BASE["hop1"], 0)
            act.wait_ge(folded, 1)
            act.activation(by_half(cur[:, :])[:, :, :, :], node_psum(4), ACT.Tanh).then_inc(x_ready, 1)
            features(0)
            evac(BASE["ode"], 1)
            act.wait_ge(folded, 2)
            act.activation(by_half(scr_a), node_psum(4), ACT.Tanh).then_inc(tanh_done, 1)
            layernorm_root()
            evac(BASE["decay0"], 2)
            layernorm_root()
            features(1)
            for q in range(2):
                def relu(k, i, q=q):
                    act.wait_ge(decay_used, i * RING + (q * NB + k + 1))
                    for c, (o, w) in enumerate(QUART_CHUNKS):
                        act.wait_ge(tri_done, i * (4 * RING) + (4 * (q * NB + k) + 2 * c + 1))
                        dst = decay[k % 2].bitcast(I16)[:, o:o + w]
                        act.activation(dst, bank(c, w), ACT.Relu).then_inc(relu_act, 1)
                each_block(act, relu)
            act.wait_ge(decay_used, 2 + 2 * NB)
            act.activation(agg_f[:, 0:QUART], bank(4, QUART), ACT.Copy).then_inc(evac_act, 1)
            layernorm_root()

            for it in range(2):
                features(2 + it)
                root(small["structural"][:, :], small["imp"][:, :], struct_sq, it + 1, struct_done)
                act.wait_ge(dup_psum, 3 * it + 1)
                act.wait_ge(parts, it + 1)
                act.activation(full, ps[:, 0:NP], ACT.Identity, bias=tiny["query_shift"][:, :], scale=D ** -0.5)\
                    .then_inc(query_f32, 1)
                act.wait_ge(query_f32, it + 1)
                act.activation(part1, full, ACT.Copy).then_inc(cut_act, 1)
                evac(BASE[f"att{it}"], 4 + 3 * it)
                act.wait_ge(dup_psum, 3 * it + 2)
                act.wait_ge(cut_ready, 3 * it + 1)
                act.activation(part1, ps[:, 0:NP], ACT.Copy).then_inc(cut_act, 1)

                def exps(k, i, g):
                    act.wait_ge(negmax_ready, i * RING + (g * NB + k + 1))
                    act.activation(prod[k % 2][:, 0:N], prod[k % 2][:, 0:N], ACT.Exp, bias=negmax[:, k % 2:k % 2 + 1],
                                   accum_out=rowsum[:, k % 2:k % 2 + 1]).then_inc(exp_done, 1)
                each_block(act, lambda k, i: exps(k, i, 2 * it))

                def node_exp(r):
                    act.wait_ge(soft_bias, r + 1)
                    act.activation(small["node_e"][:, :], small["node_z"][:, :], ACT.Exp, bias=tiny["ngmax"][:, :],
                                   accum_out=tiny["psum_"][:, :]).then_inc(part_sum, 1)
                node_exp(2 * it)
                root(small["norm"][:, :], small["rnorm"][:, :], norm_sq, it + 1, norm_rt)
                act.wait_ge(dup_psum, 3 * it + 3)
                act.wait_ge(cut_ready, 3 * it + 2)
                act.activation(part1, ps[:, 0:NP], ACT.Copy).then_inc(cut_act, 1)

                def exp_and_sign(k, i):
                    g = 2 * it + 1
                    exps(k, i, g)
                    act.wait_ge(negcut_ready, i * RING + (it * NB + k + 1))
                    at = i * (RING * NP) + k * NP
                    act.activation(signs[:, bass.ds(at, N)], prod[k % 2][:, 0:N], ACT.Sign,
                                   bias=negcut[:, k % 2:k % 2 + 1]).then_inc(product_free, 1)
                act.wait_ge(cut_ready, 3 * it + 3)
                each_block(act, exp_and_sign)
                node_exp(2 * it + 1)
                root(small["dv"][:, :], small["node_z"][:, :], deg_sq, it + 1, deg_rt)
                evac(BASE[f"up{it}"], 5 + 3 * it)

                act.wait_ge(down_ready, it + 1)

                def columns(k, i):
                    act.wait_ge(signs_t, i * (4 * RING) + (4 * (it * NB + k) + 4))
                    at = i * (RING * P) + k * P
                    dst = sign_cols[k % 2].rearrange("p (b n) -> p b n", b=NB)
                    act.activation(dst, signs3[:, :, bass.ds(at, P)], ACT.Copy).then_inc(col_ready, 1)
                each_block(act, columns)
                evac(BASE[f"up{it}"] + NB, 6 + 3 * it)
                if it == 1:
                    layernorm_root()

        @block.vector
        def _(dve):
            links = [0]

            def link(ins):
                links[0] += 1
                ins.then_inc(dve_chain, 1)
                dve.wait_ge(dve_chain, links[0])

            def evac(n_done, cols=HALF - 2 * BANK):
                dve.wait_ge(block_done, RING + n_done)
                dve.tensor_copy(agg_f[:, 2 * BANK:HALF], ps[:, 2 * BANK:HALF]).then_inc(evac_dve, 1)

            def features(r):
                dve.wait_ge(xt_psum, r + 1)
                dve.tensor_copy(xt[:, 2 * BANK:HALF], ps[:, 2 * BANK:HALF]).then_inc(xt_dve, 1)

            lns = [0]

            def layernorm():
                s, q = blocks3(scr_a), blocks3(scr_b)
                mean = small["mean"]
                link(dve.tensor_reduce(mean[:, :], s, axis=X, op=ALU.add))
                link(dve.tensor_scalar(mean[:, :], mean[:, :], 1.0 / D, None, ALU.mult))
                link(dve.tensor_tensor(s, s, per_node(mean[:, :]), ALU.subtract))
                link(dve.tensor_tensor(q, s, s, ALU.mult))
                link(dve.tensor_reduce(mean[:, :], q, axis=X, op=ALU.add))
                dve.tensor_scalar(mean[:, :], mean[:, :], 1.0 / D, None, ALU.mult).then_inc(ln_var, 1)
                lns[0] += 1
                dve.wait_ge(ln_sd, lns[0])
                link(dve.reciprocal(small["var"][:, :], small["var"][:, :]))
                return dve.tensor_tensor(blocks3(cur[:, :]), s, per_node(small["var"][:, :]), ALU.mult)

            dve.wait_ge(const_loaded, 7 * 16)
            dve.tensor_copy(ident_b[:, :], ident).then_inc(consts_cast, 1)
            dve.tensor_copy(tri, rest[:, 0:P]).then_inc(consts_cast, 1)
            dve.tensor_copy(rest_tri, rest[:, P:2 * P]).then_inc(consts_cast, 1)

            evac(BASE["hop1"])
            features(0)
            evac(BASE["ode"])
            dve.wait_ge(tanh_done, 1)
            link(dve.tensor_tensor(scr_a, scr_a, xw[:, :], ALU.add))
            layernorm().then_inc(x_ready, 1)

            evac(BASE["decay0"])
            dve.wait_ge(folded, 3)
            dve.wait_ge(x_ready, 2)
            link(dve.tensor_tensor(by_half(scr_b), node_psum(4), by_half(cur[:, :]), ALU.mult))
            link(dve.tensor_reduce(small["mean"][:, :], blocks3(scr_b), axis=X, op=ALU.add))
            link(dve.tensor_scalar(small["mean"][:, :], small["mean"][:, :], 0.01, None, ALU.mult))
            link(dve.tensor_scalar(scr_a, cur[:, :], -0.1, 1.0, ALU.mult, ALU.add))
            link(dve.tensor_tensor(blocks3(scr_a), blocks3(scr_a), per_node(small["mean"][:, :]), ALU.subtract))
            link(dve.tensor_tensor(scr_a, scr_a, cur[:, :], ALU.add))
            layernorm().then_inc(x_ready, 1)

            features(1)
            dve.wait_ge(support_psum, 1)
            sup = support3.rearrange("p (b c d) -> p b c d", c=3, d=D)
            link(dve.tensor_scalar(by_half(scr_a), node_psum(4), float(1 << DECAY_SHIFT), None, ALU.mult))
            link(dve.tensor_copy(sup[:, :, 0], blocks3(scr_a)))
            link(dve.tensor_tensor(blocks3(scr_a), blocks3(scr_a), sup[:, :, 0], ALU.subtract))
            link(dve.tensor_copy(sup[:, :, 1], blocks3(scr_a)))
            dve.tensor_tensor(sup[:, :, 2], blocks3(scr_a), sup[:, :, 1], ALU.subtract).then_inc(support_ready, 1)

            for q in range(2):
                def mask_of(k, i, q=q):
                    slot = landed(dve, f"decay{q}", k, i)
                    dve.wait_ge(decay_used, i * RING + (q * NB + k + 1))
                    dve.tensor_scalar(nbr[k % 2], slot[:, 0:2 * QUART], 0.0, None, ALU.not_equal).then_inc(block_done, 1)

                def relu(k, i, q=q):
                    for c, (o, w) in enumerate(QUART_CHUNKS):
                        dve.wait_ge(tri_done, i * (4 * RING) + (4 * (q * NB + k) + 2 * c + 2))
                        dst = decay[k % 2].bitcast(I16)[:, QUART + o:QUART + o + w]
                        dve.tensor_scalar(dst, bank(2 + c, w), 0.0, None, ALU.max).then_inc(relu_dve, 1)

                def step(k, i):
                    mask_of(k, i)
                    relu(k, i)
                each_block(dve, step)
            dve.wait_ge(decay_used, 2 + 2 * NB)
            dve.tensor_copy(agg_f[:, QUART:HALF], bank(6, QUART)).then_inc(evac_dve, 1)
            dve.wait_ge(folded, 4)
            link(dve.tensor_tensor(by_half(scr_a), node_psum(0), by_half(cur[:, :]), ALU.add))
            link(dve.tensor_tensor(by_half(scr_a), by_half(scr_a), per_feature4(decay_bias), ALU.add))
            link(layernorm())
            dve.tensor_scalar(cur[:, (NB - 1) * D:NB * D], cur[:, (NB - 1) * D:NB * D], real[:, NB - 1:NB], None,
                              ALU.mult).then_inc(x_ready, 1)

            def cut_parts(source, d12, d21, d31, d13, n_act, after=None):
                dve.wait_ge(cut_act, n_act)
                link(dve.tensor_tensor(rest, source, part1, ALU.subtract))
                link(dve.tensor_copy(part2, rest))
                link(dve.tensor_tensor(part3, rest, part2, ALU.subtract))
                lo, hi = slice(0, D), slice(D, P)
                for dst, first, second in ((d12, part1, part2), (d21, part2, part1), (d31, part3, part1),
                                           (d13, part1, part3)):
                    if dst is not None:
                        dve.tensor_copy(dst[lo, :], first[lo, :])
                        last = dve.tensor_copy(dst[hi, :], second[hi, :])
                last.then_inc(cut_ready, 1)

            def product_pieces(name, k, i):
                g = PRODUCTS.index(name)
                slot = landed(dve, name, k, i)
                dve.wait_ge(product_free, i * RING + (g * NB + k + 1))
                for c, (o, w) in enumerate(PIECES):
                    w = min(w, N - o)
                    buf = (k + c) % 2
                    dve.wait_ge(piece_ready, i * (3 * RING) + ((g * NB + k) * 3 + c + 1))
                    dve.memset(gates[:, 3 * (k % 2) + c:3 * (k % 2) + c + 1], 0.0)
                    dve.tensor_tensor_reduce(out=prod[k % 2][:, o:o + w], in0=bank(3 * buf, w), in1=slot[:, o:o + w],
                                             scale=1.0, scalar=-3.0e38, op0=ALU.mult, op1=ALU.max,
                                             accum_out=max3[:, 3 * (k % 2) + c:3 * (k % 2) + c + 1])\
                        .then_inc(piece_read, 1)
                dve.wait_ge(piece_read, i * (3 * RING) + ((g * NB + k) * 3 + 3 + 2))
                red = dve.tensor_reduce(rowmax[:, k % 2:k % 2 + 1], max3[:, 3 * (k % 2):3 * (k % 2) + 3], axis=X, op=ALU.max)
                if name.startswith("att"):
                    red.then_inc(block_done, 1)
                    dve.wait_ge(block_done, i * RING + (BASE[name] + k + 1 + RING))
                else:
                    red.then_inc(rowmax_done, 1)
                    dve.wait_ge(rowmax_done, i * RING + (g // 2 * NB + k + 1))
                dve.tensor_scalar(negmax[:, k % 2:k % 2 + 1], rowmax[:, k % 2:k % 2 + 1], -1.0, None, ALU.mult)\
                    .then_inc(negmax_ready, 1)

            def product_pass(name, after):
                product_pieces(name, 0, 0)
                product_pieces(name, 1, 0)
                after(0, 0)
                with dve.Fori(0, NB // RING) as i:
                    for k in range(2, 2 + RING):
                        product_pieces(name, k, i)
                        after(k - 1, i)
                after(NB % RING - 1 + RING, NB // RING - 1)

            def column_sums(g, dst):
                dve.wait_ge(colsum_psum, g + 1)
                dve.tensor_copy(col_rows, ps[:, 6 * BANK:8 * BANK]).then_inc(colsum_sbuf, 1)
                dve.wait_ge(colsum_t, g + 1)
                for h, rows_, cols in ((0, (0, 4), 4), (1, (0, 2), 4), (1, (2, 3), 2)):
                    v = bank(h).rearrange("p (s r z) -> p r s z", r=4, z=32)[:, rows_[0]:rows_[1], 0:cols, 0]
                    at = 16 * h + 4 * rows_[0]
                    o = dst[:, at:at + (rows_[1] - rows_[0]) * cols].rearrange("p (r s) -> p r s", s=cols)
                    last = dve.tensor_copy(o, v)
                return last

            def node_softmax(r, threshold, dst):
                dve.tensor_reduce(tiny["pmax"][:, :], small["node_z"][:, :], axis=X, op=ALU.max).then_inc(part_max, 1)
                dve.wait_ge(all_max, r + 1)
                dve.tensor_scalar(tiny["ngmax"][:, :], tiny["gmax"][:, :], -1.0, None, ALU.mult).then_inc(soft_bias, 1)
                dve.wait_ge(all_sum, r + 1)
                link(dve.tensor_scalar(tiny["thr"][:, :], tiny["gsum"][:, :], threshold, None, ALU.mult))
                link(dve.tensor_scalar(dst, small["node_e"][:, :], tiny["thr"][:, :], None, ALU.is_ge))

            for it in range(2):
                th_comp, th_edge, th_node = thresholds(it)
                S = {n: t[:, :] for n, t in small.items()}
                features(2 + it)
                dve.wait_ge(proj_psum, 2 * it + 1)
                dve.tensor_copy(by_half(xw[:, :]), node_psum(4)).then_inc(proj_read, 1)
                dve.wait_ge(proj_psum, 2 * it + 2)
                dve.tensor_tensor(by_half(scr_a), node_psum(0), per_feature4(value_bias), ALU.add).then_inc(value_ready, 1)
                dve.tensor_scalar(tiny["query_shift"][:, :], query_bias, D ** -0.5, None, ALU.mult).then_inc(parts, 1)
                dve.wait_ge(proj_read, it + 1)
                link(dve.tensor_tensor(scr_b, xw[:, :], xw[:, :], ALU.mult))
                link(dve.tensor_reduce(S["imp"], blocks3(scr_b), axis=X, op=ALU.add))
                dve.tensor_scalar(S["imp"], S["imp"], 1e-16, None, ALU.max).then_inc(struct_sq, 1)
                dve.wait_ge(query_f32, it + 1)
                cut_parts(full, query12, None, None, query13, 3 * it + 1)
                evac(BASE[f"att{it}"])
                dve.wait_ge(dup_psum, 3 * it + 2)
                cut_parts(ps[:, 0:NP], right12, right21, right31, None, 3 * it + 2)

                def weigh(k, i):
                    dve.wait_ge(exp_done, i * RING + (2 * it * NB + k + 1))
                    dve.reciprocal(rowmax[:, k % 2:k % 2 + 1], rowsum[:, k % 2:k % 2 + 1]).then_inc(rz_done, 1)
                    dve.wait_ge(rz_done, i * RING + (it * NB + k + 1))
                    dve.tensor_scalar(rz32[:, k % 2 * 32:(k % 2 + 1) * 32], ones32[:, :], rowmax[:, k % 2:k % 2 + 1],
                                      real[:, bass.ds(i * RING + k, 1)], ALU.mult, ALU.mult).then_inc(rz_ready, 1)
                product_pass(f"att{it}", weigh)
                link(column_sums(2 * it, S["colsum"]))
                dve.wait_ge(struct_done, it + 1)
                link(dve.tensor_scalar(S["imp"], S["structural"], 0.5, None, ALU.mult))
                link(dve.scalar_tensor_tensor(out=S["imp"], in0=S["colsum"], scalar=0.5 / N, in1=S["imp"],
                                              op0=ALU.mult, op1=ALU.add))
                link(dve.tensor_tensor(S["imp"], S["imp"], real, ALU.mult))
                link(dve.tensor_tensor(S["node_z"], S["imp"], not_real, ALU.add))
                node_softmax(2 * it, th_comp, S["comp"])
                link(dve.tensor_scalar(S["blocked"], S["comp"], -HUGE, HUGE, ALU.mult, ALU.add))
                if it == 0:
                    dve.wait_ge(kept_read, 1)
                link(dve.tensor_tensor(blocks3(scr_a), blocks3(cur[:, :]), per_node(S["comp"]), ALU.mult))
                link(dve.tensor_tensor(scr_b, scr_a, scr_a, ALU.mult))
                link(dve.tensor_reduce(S["rnorm"], blocks3(scr_b), axis=X, op=ALU.add))
                dve.tensor_scalar(S["rnorm"], S["rnorm"], 1e-16, None, ALU.max).then_inc(norm_sq, 1)
                dve.wait_ge(norm_rt, it + 1)
                link(dve.tensor_scalar(S["rnorm"], S["norm"], 1e-8, None, ALU.max))
                link(dve.reciprocal(S["rnorm"], S["rnorm"]))
                dve.tensor_tensor(blocks3(scr_a), blocks3(scr_a), per_node(S["rnorm"]), ALU.mult).then_inc(normed, 1)
                dve.wait_ge(dup_psum, 3 * it + 3)
                cut_parts(ps[:, 0:NP], right12, right21, right31, cos13, 3 * it + 3)

                def prune(k, i):
                    dve.wait_ge(exp_done, i * RING + ((2 * it + 1) * NB + k + 1))
                    one = slice(k % 2, k % 2 + 1)
                    at = bass.ds(i * RING + k, 1)
                    dve.scalar_tensor_tensor(out=cut[:, one], in0=rowsum[:, one], scalar=th_edge,
                                             in1=S["blocked"][:, at], op0=ALU.mult, op1=ALU.add).then_inc(cut_done, 1)
                    dve.wait_ge(cut_done, i * RING + (it * NB + k + 1))
                    dve.tensor_scalar(negcut[:, one], cut[:, one], -1.0, None, ALU.mult).then_inc(negcut_ready, 1)
                    slot = slot_of(f"cos{it}", k)
                    dve.scalar_tensor_tensor(out=slot[:, 0:N], in0=prod[k % 2][:, 0:N], scalar=cut[:, one],
                                             in1=slot[:, 0:N], op0=ALU.is_ge, op1=ALU.mult,
                                             accum_out=S["conn"][:, at]).then_inc(pruned, 1)
                product_pass(f"cos{it}", prune)

                link(dve.memset(signs3[:, :, N:NP], 0))
                link(column_sums(2 * it + 1, S["edeg"]))
                link(dve.tensor_scalar(S["edeg"], S["edeg"], 1e-6, None, ALU.max))
                link(dve.reciprocal(S["edeg"], S["edeg"]))
                link(dve.tensor_tensor(S["imp"], S["conn"], S["norm"], ALU.mult))
                link(dve.tensor_tensor(S["imp"], S["imp"], real, ALU.mult))
                link(dve.tensor_tensor(S["node_z"], S["imp"], not_real, ALU.add))
                node_softmax(2 * it + 1, th_node, S["imp"])
                link(dve.scalar_tensor_tensor(out=S["imp"], in0=S["conn"], scalar=0.0, in1=S["imp"],
                                              op0=ALU.is_gt, op1=ALU.mult))
                link(dve.tensor_tensor(S["imp"], S["imp"], S["comp"], ALU.mult))
                dve.tensor_scalar(S["node_z"], S["conn"], 1e-6, None, ALU.max).then_inc(deg_sq, 1)
                dve.wait_ge(deg_rt, it + 1)
                link(dve.reciprocal(S["dv"], S["dv"]))
                link(dve.tensor_tensor(S["imp"], S["imp"], S["dv"], ALU.mult))
                dve.tensor_tensor(blocks3(cur[:, :]), blocks3(xw[:, :]), per_node(S["imp"]), ALU.mult)\
                    .then_inc(down_ready, 1)

                def down(k, i):
                    slot = landed(dve, f"down{it}", k, i)
                    at = i * (RING * NP) + k * NP
                    dve.scalar_tensor_tensor(out=slot[:, 0:N], in0=signs[:, bass.ds(at, N)], scalar=0.0,
                                             in1=slot[:, 0:N], op0=ALU.is_ge, op1=ALU.mult).then_inc(pruned, 1)
                each_block(dve, down)
                evac(BASE[f"up{it}"])
                dve.wait_ge(folded, 5 + 2 * it)
                dve.tensor_tensor(by_half(cur[:, :]), node_psum(4), per_node4(S["edeg"]), ALU.mult).then_inc(up_ready, 1)

                def up(k, i):
                    slot = landed(dve, f"up{it}", k, i)
                    v = slot[:, :].rearrange("p (h n) -> p h n", h=2)
                    for c, (o, w) in enumerate(HALF_CHUNKS):
                        dve.wait_ge(signs_t, i * (4 * RING) + (4 * (it * NB + k) + c + 9))
                        b = 4 + 2 * (c % 2)
                        s = ps[:, b * BANK:(b + 2) * BANK].rearrange("p (h n) -> p h n", h=2)[:, :, 0:w]
                        dve.scalar_tensor_tensor(out=v[:, :, o:o + w], in0=s, scalar=0.0, in1=v[:, :, o:o + w],
                                                 op0=ALU.is_ge, op1=ALU.mult).then_inc(up_pruned, 1)
                each_block(dve, up)
                evac(BASE[f"up{it}"] + NB)
                dve.wait_ge(folded, 6 + 2 * it)
                link(dve.tensor_tensor(by_half(scr_a), node_psum(4), per_node4(S["dv"]), ALU.mult))
                if it == 0:
                    dve.tensor_scalar(cur[:, :], scr_a, 0.0, None, ALU.max).then_inc(x_ready, 1)
                else:
                    dve.wait_ge(kept, 32)
                    link(dve.scalar_tensor_tensor(out=scr_a, in0=scr_a, scalar=0.0, in1=xw[:, :],
                                                  op0=ALU.max, op1=ALU.add))
                    layernorm().then_inc(out_ready, 1)


def kernel(x, adj, L0_gnn_W, L1_gnn_t, L2_gnn_weight, L2_gnn_bias, L3_gnn_W, L3_gnn_Theta, L3_gnn_Wq, L3_gnn_bq,
           L3_gnn_Wv, L3_gnn_bv):
    import concourse.bacc as bacc
    from concourse.bass_utils import run_bass_kernel_spmd

    def f(a):
        return np.asarray(a)

    def nodes(a):
        return np.ascontiguousarray(a.reshape(NB, P, -1).transpose(1, 0, 2).reshape(P, -1))

    x, adj = f(x), f(adj)
    xp = np.zeros((NP, D), np.float32)
    xp[:N] = x
    ap = np.zeros((NP, NP), np.float32)
    ap[:N, :N] = adj
    x_feat = np.ascontiguousarray(xp.T.reshape(D, 2, HALF).transpose(1, 0, 2).reshape(P, HALF))
    w0 = f(L0_gnn_W)
    mats = [w0[0, :D], w0[0, D:], w0[1, :D], w0[1, D:], f(L2_gnn_weight), f(L3_gnn_W), f(L3_gnn_Theta), f(L3_gnn_Wv),
            f(L3_gnn_Wq), f(L3_gnn_Wq)]
    weights = np.concatenate([np.concatenate([m, m], 0) for m in mats], 1)
    rows = np.concatenate([np.broadcast_to(f(b)[None], (P, D)) for b in (L2_gnn_bias, L3_gnn_bv)], 1)
    bq = np.concatenate([f(L3_gnn_bq)] * 2)[:, None]
    eye = np.eye(P, dtype=np.float32)
    twice = np.tile(np.eye(D, dtype=np.float32), (2, 2))
    real = np.ones((P, NB), np.float32)
    real[N - (NB - 1) * P:, NB - 1] = 0
    consts = np.concatenate([eye, twice, real, np.where(real > 0, 0, -HUGE).astype(np.float32)], 1)
    later = np.tri(P, P, -1, dtype=np.float32)
    tri = -P * later + MARK * eye
    decay_consts = np.concatenate([tri, -P - tri], 1)

    arrays = {"adj": ap, "adj_t": np.ascontiguousarray(ap.T), "x_nodes": nodes(xp), "x_feat": x_feat,
              "weights": weights, "rows": rows, "bq": bq, "consts": consts, "decay_consts": decay_consts}
    arrays = {n: np.ascontiguousarray(a) for n, a in arrays.items()}
    nc = bacc.Bacc("TRN2", target_bir_lowering=False, num_devices=1)
    args = [nc.dram_tensor(n, a.shape, F32, kind="ExternalInput").ap() for n, a in arrays.items()]
    kept = nc.dram_tensor("x_kept", (P, NB * D), F32, kind="Internal").ap()
    out = nc.dram_tensor("out", (P, NB, D), F32, kind="ExternalOutput").ap()
    build_program(nc, *args, kept, out)
    r = run_bass_kernel_spmd(nc, [arrays], core_ids=[0])
    got = r.results[0]["out"]
    return np.ascontiguousarray(got.transpose(1, 0, 2).reshape(NP, D)[:N])
```

```python
from contextlib import ExitStack

import concourse.bass as bass
import numpy as np
from concourse import mybir

F32 = mybir.dt.float32
BF16 = mybir.dt.bfloat16
I16 = mybir.dt.int16
I8 = mybir.dt.int8
ALU = mybir.AluOpType
ACT = mybir.ActivationFunctionType
X = mybir.AxisListType.X
RMAX = bass.bass_isa.ReduceOp.max
RADD = bass.bass_isa.ReduceOp.add

N = 3327
D = 64
P = 128
NB = (N + P - 1) // P
NP = NB * P
HALF = NP // 2
HB = NB // 2
RING = 4
BANK = 512
HALF_CHUNKS = [(o, min(BANK, HALF - o)) for o in range(0, HALF, BANK)]
QUART = HALF // 2
QUART_CHUNKS = [(o, min(BANK, QUART - o)) for o in range(0, QUART, BANK)]
PIECE = 9 * P
PIECES = [(o, min(PIECE, NP - o)) for o in range(0, NP, PIECE)]
ROW_CHUNKS = [(o, min(BANK, NP - o)) for o in range(0, NP, BANK)]
LO, HI = slice(0, D), slice(D, P)
LN_EPS = 1e-5
HUGE = 1e30
NEIGHBOURS = 100
DECAY_SHIFT = 27
MARK = 1 << 14
THETA0, THETA_MAX, LAM = 0.000244, 0.0003, 0.1
WEIGHTS = ["w0_agg", "w0_self", "w1_agg", "w1_self", "decay_w", "hyper_w", "theta", "value_w", "query_w", "query_w2"]

PASSES = [("hop0", NB), ("hop1", NB), ("ode", NB), ("decay0", NB), ("decay1", NB)]
for _it in range(2):
    PASSES += [(f"{s}{_it}", NB) for s in ("edge", "att", "cos", "down", "up")]
BASE = {}
_n = 0
for _name, _count in PASSES:
    BASE[_name] = _n
    _n += _count
AGGS = ["hop0", "hop1", "ode", "decay", "edge0", "down0", "up0", "edge1", "down1", "up1"]
PRODUCTS = ["att0", "cos0", "att1", "cos1"]


def thresholds(it):
    base = THETA0 + (1.0 - np.exp(-LAM * it)) * (THETA_MAX - THETA0)
    return float(base), float(min(base, 0.8)), float(min(base, 0.7))


def build_program(nc, adj, adj_t, x_nodes, x_feat, weights, rows, bq, consts, decay_consts, x_kept, out):
    ctx = ExitStack()
    with ctx:
        def sb(name, cols, dt):
            return ctx.enter_context(nc.sbuf_tensor(name, [P, cols], dt))

        def sem(name):
            return ctx.enter_context(nc.semaphore(name))

        slots = [sb(f"slot{i}", NP, F32) for i in range(RING)]
        arena = sb("arena", NB * NP // 4, F32)
        signs = arena[:, :].bitcast(I8)
        signs3 = signs.rearrange("p (b n) -> p b n", b=NB)
        pairs = sb("pairs", 2 * NP, F32)
        prod = [pairs[:, i * NP:(i + 1) * NP] for i in range(2)]
        agg_f = pairs[:, 0:HALF]
        col_rows = pairs[:, HALF:HALF + 2 * BANK]
        xw = sb("xw", NB * D, F32)
        cur = sb("cur", NB * D, F32)
        right12 = sb("right12", NP, BF16)
        right21 = sb("right21", NP, BF16)
        right31 = sb("right31", NP, BF16)
        cos13 = cur[:, :].bitcast(BF16)

        off = [0]

        def work(words):
            a = arena[:, off[0]:off[0] + words]
            off[0] += words
            return a
        xt = work(HALF)
        scr_a = work(NB * D)
        scr_b = work(NB * D)
        full = work(NP)
        rest = work(NP)
        part1 = work(NP // 2).bitcast(BF16)
        part2 = work(NP // 2).bitcast(BF16)
        part3 = work(NP // 2).bitcast(BF16)
        query12 = work(NP // 2).bitcast(BF16)
        query13 = work(NP // 2).bitcast(BF16)
        assert off[0] <= NB * NP // 4
        hat12, hat21 = (full[:, i * NP // 2:(i + 1) * NP // 2].bitcast(BF16) for i in range(2))
        hat31, hat13 = (rest[:, i * NP // 2:(i + 1) * NP // 2].bitcast(BF16) for i in range(2))
        support3 = full.bitcast(BF16)[:, 0:NB * 3 * D]
        nbr = [pairs[:, HALF + i * QUART:HALF + (i + 1) * QUART].bitcast(BF16) for i in range(4)]
        decay = [pairs[:, HALF + (4 + i) * QUART:HALF + (5 + i) * QUART] for i in range(2)]
        tri = right31[:, 0:P]
        rest_tri = right31[:, P:2 * P]
        start_bits = right31[:, 2 * P:3 * P]
        stat3 = [right31[:, (3 + 2 * i) * P:(3 + 2 * i) * P + 3 * D] for i in range(2)]
        sign_cols = [right12[:, :], right21[:, :]]

        wt = sb("wt", len(WEIGHTS) * D, F32)
        W = {n: wt[:, i * D:(i + 1) * D] for i, n in enumerate(WEIGHTS)}
        rowt = sb("rowt", 2 * D + 1, F32)
        decay_bias, value_bias, query_bias = rowt[:, 0:D], rowt[:, D:2 * D], rowt[:, 2 * D:2 * D + 1]
        cst = sb("cst", 2 * P + 2 * NB, F32)
        ident, twice = cst[:, 0:P], cst[:, P:2 * P]
        real, not_real = cst[:, 2 * P:2 * P + NB], cst[:, 2 * P + NB:2 * P + 2 * NB]
        ident_b = sb("ident_b", P, BF16)
        zeros_b = sb("zeros_b", P, BF16)
        ones_b = sb("ones_b", BANK, BF16)
        ones32 = sb("ones32", 32, F32)
        stat = sb("stat", 2 * D, F32)
        rz32 = sb("rz32", 2 * 32, F32)
        small = {n: sb(n, NB, F32) for n in
                 ("mean", "var", "structural", "colsum", "imp", "comp", "blocked", "norm", "rnorm",
                  "conn", "node_z", "node_e", "dv", "edeg")}
        tiny = {n: sb(n, 1, F32) for n in ("pmax", "gmax", "ngmax", "psum_", "gsum", "thr", "query_shift")}
        max3 = sb("max3", 2 * 3, F32)
        rowmax = sb("rowmax", 2, F32)
        gates = sb("gates", 6, F32)
        negmax = sb("negmax", 2, F32)
        rowsum = sb("rowsum", 2, F32)
        cut = sb("cut", 2, F32)
        negcut = sb("negcut", 2, F32)
        eps_t = sb("eps_t", 1, F32)

        ps = ctx.enter_context(nc.psum_tensor("ps", [P, 8 * BANK], F32))

        def bank(b, cols=BANK, at=0):
            return ps[:, b * BANK + at:b * BANK + at + cols]

        def by_half(t):
            return t.rearrange("p (h b d) -> p h b d", h=2, d=D)

        def node_psum(first):
            v = ps[:, first * BANK:(first + 4) * BANK].rearrange("p (h n) -> p h n", h=2)
            return v[:, :, 0:HB * D].rearrange("p h (b d) -> p h b d", d=D)

        def halves_psum():
            return ps[:, :].rearrange("p (h n) -> p h n", h=2)[:, :, 0:HALF]

        def two(t):
            return t.rearrange("p (h n) -> p h n", h=2)

        def per_node(t):
            return t.unsqueeze(2).to_broadcast([P, NB, D])

        def per_node4(t):
            return t.rearrange("p (h b) -> p h b", h=2).unsqueeze(3).to_broadcast([P, 2, HB, D])

        def per_feature4(t):
            return t.unsqueeze(1).unsqueeze(1).to_broadcast([P, 2, HB, D])

        def stacked(t):
            return t.rearrange("p (b c d) -> p b c d", c=2, d=D)

        def blocks3(t):
            return t.rearrange("p (b d) -> p b d", d=D)

        slot_loaded = [sem(f"slot_loaded{i}") for i in range(RING)]
        block_done = sem("block_done")
        stat_ready = sem("stat_ready")
        const_loaded = sem("const_loaded")
        consts_made = sem("consts_made")
        consts_cast = sem("consts_cast")
        evac_act = sem("evac_act")
        evac_dve = sem("evac_dve")
        folded = sem("folded")
        x_ready = sem("x_ready")
        xt_psum = sem("xt_psum")
        xt_act = sem("xt_act")
        xt_dve = sem("xt_dve")
        dve_chain = sem("dve_chain")
        ln_var = sem("ln_var")
        ln_sd = sem("ln_sd")
        tanh_done = sem("tanh_done")
        support_psum = sem("support_psum")
        support_ready = sem("support_ready")
        tri_done = sem("tri_done")
        relu_act = sem("relu_act")
        relu_dve = sem("relu_dve")
        decay_used = sem("decay_used")
        kept = sem("kept")
        kept_read = sem("kept_read")
        proj_psum = sem("proj_psum")
        proj_read = sem("proj_read")
        struct_sq = sem("struct_sq")
        struct_done = sem("struct_done")
        query_f32 = sem("query_f32")
        parts = sem("parts")
        cut_act = sem("cut_act")
        stack_act = sem("stack_act")
        cut_ready = sem("cut_ready")
        hat_parts = sem("hat_parts")
        hat_stacked = sem("hat_stacked")
        hat_psum = sem("hat_psum")
        hat_dve = sem("hat_dve")
        hat_act = sem("hat_act")
        query_half = sem("query_half")
        value_psum = sem("value_psum")
        dup_psum = sem("dup_psum")
        piece_ready = sem("piece_ready")
        piece_read = sem("piece_read")
        rowmax_done = sem("rowmax_done")
        negmax_ready = sem("negmax_ready")
        exp_done = sem("exp_done")
        rz_done = sem("rz_done")
        rz_ready = sem("rz_ready")
        cut_done = sem("cut_done")
        negcut_ready = sem("negcut_ready")
        pruned = sem("pruned")
        product_free = sem("product_free")
        colsum_psum = sem("colsum_psum")
        colsum_sbuf = sem("colsum_sbuf")
        colsum_t = sem("colsum_t")
        part_max = sem("part_max")
        all_max = sem("all_max")
        part_sum = sem("part_sum")
        all_sum = sem("all_sum")
        soft_bias = sem("soft_bias")
        norm_sq = sem("norm_sq")
        norm_rt = sem("norm_rt")
        deg_sq = sem("deg_sq")
        deg_rt = sem("deg_rt")
        down_ready = sem("down_ready")
        up_ready = sem("up_ready")
        value_ready = sem("value_ready")
        col_ready = sem("col_ready")
        signs_t = sem("signs_t")
        up_pruned = sem("up_pruned")
        out_ready = sem("out_ready")
        stored = sem("stored")

        block = ctx.enter_context(nc.Block())

        def each_block(eng, body):
            head = NB % RING
            for k in range(head):
                body(k, 0)
            with eng.Fori(0, NB // RING) as i:
                for k in range(head, head + RING):
                    body(k, i)

        def landed(eng, name, k, i):
            n = BASE[name] + k
            eng.wait_ge(slot_loaded[n % RING], (n // RING + i + 1) * 16)
            return slots[n % RING]

        def slot_of(name, k):
            return slots[(BASE[name] + k) % RING]

        @block.sync
        def _(sp):
            sp.dma_start(xw[:, :], x_nodes).then_inc(const_loaded, 16)
            sp.dma_start(xt, x_feat).then_inc(const_loaded, 16)
            sp.dma_start(cst[:, :], consts).then_inc(const_loaded, 16)
            sp.dma_start(wt[:, :], weights).then_inc(const_loaded, 16)
            sp.dma_start(rowt[:, 0:2 * D], rows).then_inc(const_loaded, 16)
            sp.dma_start(rowt[:, 2 * D:2 * D + 1], bq).then_inc(const_loaded, 16)
            sp.dma_start(rest[:, 0:2 * P], decay_consts).then_inc(const_loaded, 16)

            def stream(name, source, quarter=None):
                def load(k, i):
                    n = BASE[name] + k
                    row = i * (RING * P) + k * P if quarter is None else i * (-RING * P) + (NB - 1 - k) * P
                    row = row if isinstance(row, int) else sp.snap(row)
                    sp.wait_ge(block_done, i * RING + (n + 1))
                    slot = slots[n % RING]
                    if quarter is None:
                        src, dst = source[bass.ds(row, P), :], slot[:, :]
                    else:
                        src = source[bass.ds(row, P), :].rearrange("p (h n) -> p h n", h=2)
                        src = src[:, :, quarter * QUART:(quarter + 1) * QUART]
                        dst = slot[:, 0:2 * QUART].rearrange("p (h n) -> p h n", h=2)
                    sp.dma_start(dst, src).then_inc(slot_loaded[n % RING], 16)
                each_block(sp, load)

            stream("hop0", adj_t)
            stream("hop1", adj_t)
            stream("ode", adj_t)
            stream("decay0", adj_t, 0)
            stream("decay1", adj_t, 1)
            for it in range(2):
                if it == 0:
                    sp.wait_ge(x_ready, 4)
                    sp.dma_start(x_kept, cur[:, :]).then_inc(kept, 16)
                stream(f"edge{it}", adj)
                if it == 0:
                    sp.wait_ge(kept, 16)
                    sp.sem_inc(kept_read, 1)
                stream(f"att{it}", adj)
                stream(f"cos{it}", adj)
                stream(f"down{it}", adj)
                if it == 1:
                    sp.wait_ge(down_ready, 2)
                    sp.dma_start(xw[:, :], x_kept).then_inc(kept, 16)
                stream(f"up{it}", adj_t)
            sp.wait_ge(out_ready, 1)
            sp.dma_start(out, blocks3(cur[:, :])[:, :, :]).then_inc(stored, 16)
            sp.wait_ge(stored, 16)

        @block.gpsimd
        def _(pool):
            pool.memset(zeros_b[:, :], 0.0).then_inc(consts_made, 1)
            pool.memset(ones_b[:, :], 1.0).then_inc(consts_made, 1)
            pool.memset(ones32[:, :], 1.0).then_inc(consts_made, 1)
            pool.memset(start_bits, -float(MARK - NEIGHBOURS * P) / P).then_inc(consts_made, 1)
            pool.memset(eps_t[:, :], LN_EPS).then_inc(consts_made, 1)

            def feed(name, source):
                def copy(k, i):
                    pool.wait_ge(block_done, i * RING + (BASE[name] + k + RING - 1))
                    pool.tensor_copy(stat[:, k % 2 * D:(k % 2 + 1) * D],
                                     source[:, bass.ds(i * (RING * D) + k * D, D)]).then_inc(stat_ready, 1)
                each_block(pool, copy)

            def feed_decay(q):
                def copy(k, i):
                    pool.wait_ge(decay_used, i * RING + (q * NB + k + 3))
                    pool.tensor_copy(stat3[k % 2], support3[:, bass.ds(i * (-RING * 3 * D) + (NB - 1 - k) * 3 * D, 3 * D)])\
                        .then_inc(stat_ready, 1)
                each_block(pool, copy)

            def node_softmax(r):
                pool.wait_ge(part_max, r + 1)
                pool.partition_all_reduce(tiny["gmax"][:, :], tiny["pmax"][:, :], P, RMAX).then_inc(all_max, 1)
                pool.wait_ge(part_sum, r + 1)
                pool.partition_all_reduce(tiny["gsum"][:, :], tiny["psum_"][:, :], P, RADD).then_inc(all_sum, 1)

            pool.wait_ge(const_loaded, 7 * 16)
            feed("hop0", xw)
            pool.wait_ge(x_ready, 1)
            feed("hop1", cur)
            pool.wait_ge(x_ready, 2)
            feed("ode", cur)
            pool.wait_ge(support_ready, 1)
            feed_decay(0)
            feed_decay(1)
            for it in range(2):
                pool.wait_ge(value_ready, it + 1)
                feed(f"edge{it}", scr_a)
                node_softmax(2 * it)
                node_softmax(2 * it + 1)
                pool.wait_ge(down_ready, it + 1)
                feed(f"down{it}", cur)
                pool.wait_ge(up_ready, it + 1)
                feed(f"up{it}", cur)

        @block.tensor
        def _(pe):
            pe.sem_inc(block_done, RING)
            pe.sem_inc(piece_read, 2)
            pe.sem_inc(product_free, 2)
            pe.sem_inc(decay_used, 4)
            pe.sem_inc(signs_t, 8)
            pe.sem_inc(up_pruned, 2)
            pe.wait_ge(const_loaded, 7 * 16)
            pe.wait_ge(consts_made, 5)
            pe.wait_ge(consts_cast, 3)

            stats_before = {n: sum(2 * NB if a == "decay" else NB for a in AGGS[:AGGS.index(n)]) for n in AGGS}

            def mm(o, l, r, start=True, stop=True):
                return pe.matmul(o, l, r, start=start, stop=stop, skip_group_check=True)

            def aggregate(name, pruned_base=None):
                def step(k, i):
                    if pruned_base is None:
                        slot = landed(pe, name, k, i)
                    else:
                        slot = slot_of(name, k)
                        pe.wait_ge(pruned, i * RING + (pruned_base + k + 1))
                    pe.wait_ge(stat_ready, i * RING + (stats_before[name] + k + 1))
                    s = stat[:, k % 2 * D:(k % 2 + 1) * D]
                    for o, w in HALF_CHUNKS:
                        for h in range(2):
                            last = mm(ps[h * D:(h + 1) * D, o:o + w], s, slot[:, h * HALF + o:h * HALF + o + w],
                                      start=k == 0)
                    last.then_inc(block_done, 1)
                each_block(pe, step)

            def fold(e, right, first=4, also=None):
                pe.wait_ge(evac_act, e + 1)
                pe.wait_ge(evac_dve, e + 1)
                return to_nodes(agg_f, right, first, also)

            def to_nodes(left, right, first, also=None):
                for b in range(HB):
                    for h in range(2):
                        o = bank(first + 2 * h, at=b * D, cols=D)
                        last = mm(o, left[h * D:(h + 1) * D, b * P:(b + 1) * P], right[h * D:(h + 1) * D, :])
                        if also is not None:
                            last = mm(o, xt[h * D:(h + 1) * D, b * P:(b + 1) * P], also[h * D:(h + 1) * D, :],
                                      start=False)
                return last

            def to_features(source, first):
                for b in range(HB):
                    for h in range(2):
                        last = mm(ps[h * D:(h + 1) * D, first * BANK + b * P:first * BANK + (b + 1) * P],
                                  source[:, (h * HB + b) * D:(h * HB + b + 1) * D], ident)
                return last

            def on_both_partition_halves(left, right, h, first):
                for o, w in HALF_CHUNKS:
                    last = mm(bank(first, w, o), left[h * D:(h + 1) * D, :], right[h * D:(h + 1) * D, o:o + w])
                return last

            def to_stack(source, first):
                dst = ps[:, first * BANK:(first + 4) * BANK].bitcast(BF16)
                for b in range(NB):
                    last = pe.transpose(dst[:, b * P:(b + 1) * P], source[:, b * P:(b + 1) * P], ident_b[:, :])
                return last

            def features_round(r):
                pe.wait_ge(x_ready, r)
                to_features(cur[:, :], 0).then_inc(xt_psum, 1)

            aggregate("hop0")
            fold(0, W["w0_agg"], also=W["w0_self"]).then_inc(folded, 1)
            features_round(1)
            pe.wait_ge(xt_act, 1)
            pe.wait_ge(xt_dve, 1)
            aggregate("hop1")
            fold(1, W["w1_agg"], also=W["w1_self"]).then_inc(folded, 1)
            aggregate("ode")
            fold(2, twice[:, 0:D]).then_inc(folded, 1)
            features_round(3)
            pe.wait_ge(xt_act, 2)
            pe.wait_ge(xt_dve, 2)
            to_nodes(xt, W["decay_w"], 4).then_inc(support_psum, 1)
            pe.wait_ge(support_ready, 1)

            for q in range(2):
                if q:
                    pe.wait_ge(relu_act, 2 * NB)
                    pe.wait_ge(relu_dve, 2 * NB)
                for b in range(4):
                    mm(bank(b), start_bits, ones_b[:, :])
                for b in (4 + 2 * q, 5 + 2 * q):
                    mm(bank(b), zeros_b[:, :], ones_b[:, :])

                def marks(k):
                    return nbr[(2 * q + k) % 4]

                def own_bits(k, i, c, q=q, marks=marks):
                    if c == 0:
                        pe.wait_ge(block_done, i * RING + (BASE[f"decay{q}"] + k + 1 + RING))
                    o, w = QUART_CHUNKS[c]
                    for s in range(2):
                        mm(bank(2 * s + c, w), tri, marks(k)[:, s * QUART + o:s * QUART + o + w], start=False)\
                            .then_inc(tri_done, 1)

                def step(k, i, last_block=False, q=q, marks=marks, own_bits=own_bits):
                    dw = decay[k % 2].bitcast(BF16)
                    for c, (o, w) in enumerate(QUART_CHUNKS):
                        pe.wait_ge(relu_act, i * (2 * RING) + (2 * (q * NB + k) + c + 1))
                        pe.wait_ge(relu_dve, i * (2 * RING) + (2 * (q * NB + k) + c + 1))
                        if not last_block:
                            for s in range(2):
                                mm(bank(2 * s + c, w), rest_tri, marks(k)[:, s * QUART + o:s * QUART + o + w],
                                   start=False)
                            own_bits(k + 1, i, c)
                        if c == 0:
                            pe.wait_ge(stat_ready, i * RING + (stats_before["decay"] + q * NB + k + 1))
                        for part in range(3):
                            for s in range(2):
                                last = mm(ps[s * D:(s + 1) * D, (4 + 2 * q + c) * BANK:(4 + 2 * q + c) * BANK + w],
                                          stat3[k % 2][:, part * D:(part + 1) * D],
                                          dw[:, s * QUART + o:s * QUART + o + w], start=False)
                    last.then_inc(decay_used, 1)

                for c in range(2):
                    own_bits(0, 0, c)
                with pe.Fori(0, NB // RING) as i:
                    for k in range(RING):
                        step(k, i)
                step(NB - 2, 0)
                step(NB - 1, 0, last_block=True)
            fold(3, twice[:, 0:D], first=0).then_inc(folded, 1)

            def product(name, left12, left13):
                g = PRODUCTS.index(name)
                sums = name.startswith("att")
                for b in (6, 7):
                    mm(bank(b), zeros_b[:, :], ones_b[:, :])

                def piece(k, i, c):
                    at = i * (RING * P) + k * P
                    o, w = PIECES[c]
                    buf = (k + c) % 2
                    pe.wait_ge(piece_read, i * (RING * 3) + ((g * NB + k) * 3 + c + 1))
                    for n, (left, right) in enumerate(((left12, right12), (left12, right21), (left13, right31))):
                        for s in range(0, w, BANK):
                            v = min(BANK, w - s)
                            last = mm(bank(3 * buf, v, s), left[:, bass.ds(at, P)], right[:, o + s:o + s + v],
                                      start=n == 0)
                    last.then_inc(piece_ready, 1)

                def columns(k, i):
                    if sums:
                        pe.wait_ge(rz_ready, i * RING + (g // 2 * NB + k + 1))
                        moving, s = prod[k % 2], rz32[:, k % 2 * 32:(k % 2 + 1) * 32]
                    else:
                        pe.wait_ge(pruned, i * RING + (g // 2 * 2 * NB + k + 1))
                        moving, s = slot_of(name, k), ones32[:, :]
                    for c, (o, w) in enumerate(ROW_CHUNKS):
                        r = c % 4
                        w = min(w, N - o)
                        last = mm(ps[32 * r:32 * r + 32, (6 + c // 4) * BANK:(6 + c // 4) * BANK + w], s,
                                  moving[:, o:o + w], start=False)
                    last.then_inc(product_free if sums else block_done, 1)
                    return last

                for k in range(2):
                    for c in range(3):
                        piece(k, 0, c)
                with pe.Fori(0, NB // RING) as i:
                    for k in range(2, 2 + RING):
                        piece(k, i, 0)
                        if sums:
                            columns(k - 2, i)
                            piece(k, i, 1)
                        else:
                            piece(k, i, 1)
                            columns(k - 2, i)
                        piece(k, i, 2)
                columns(NB - 2, 0)
                columns(NB - 1, 0)
                mm(bank(0, 1), zeros_b[:, :], ones_b[:, 0:1]).then_inc(colsum_psum, 1)
                pe.wait_ge(colsum_sbuf, g + 1)
                for t in range(8):
                    last = pe.transpose(ps[:, t * P:(t + 1) * P], col_rows[:, t * P:(t + 1) * P], ident)
                last.then_inc(colsum_t, 1)

            for it in range(2):
                features_round(4 + it)
                pe.wait_ge(xt_act, 3 + it)
                pe.wait_ge(xt_dve, 3 + it)
                query = wt[:, WEIGHTS.index("query_w") * D:(WEIGHTS.index("query_w") + 2) * D]
                to_nodes(xt, W["value_w"], 0).then_inc(value_psum, 1)
                on_both_partition_halves(query, xt, 0, 4).then_inc(query_half, 1)
                pe.wait_ge(value_ready, it + 1)
                on_both_partition_halves(query, xt, 1, 0).then_inc(query_half, 1)
                pe.wait_ge(query_f32, 2 * it + 1)
                to_nodes(xt, W["hyper_w"], 4).then_inc(proj_psum, 1)
                pe.wait_ge(query_f32, 2 * it + 2)
                aggregate(f"edge{it}")
                pe.wait_ge(evac_act, 5 + 3 * it)
                pe.wait_ge(evac_dve, 5 + 3 * it)
                pe.wait_ge(proj_read, it + 1)
                for h in range(2):
                    last = on_both_partition_halves(twice, agg_f, h, 4 * h)
                last.then_inc(dup_psum, 1)
                pe.wait_ge(cut_ready, 2 * it + 2)
                product(f"att{it}", query12, query13)
                pe.wait_ge(hat_parts, 3 * it + 2)
                to_stack(hat12, 0).then_inc(hat_psum, 1)
                pe.wait_ge(hat_stacked, 2 * it + 1)
                to_stack(hat21, 4).then_inc(hat_psum, 1)
                pe.wait_ge(hat_parts, 3 * it + 3)
                pe.wait_ge(hat_dve, 2 * it + 1)
                to_stack(hat31, 0).then_inc(hat_psum, 1)
                pe.wait_ge(hat_stacked, 2 * it + 2)
                pe.wait_ge(hat_act, 2 * it + 1)
                to_stack(hat13, 4).then_inc(hat_psum, 1)
                pe.wait_ge(hat_dve, 2 * it + 2)
                pe.wait_ge(hat_act, 2 * it + 2)
                product(f"cos{it}", right12, cos13)
                aggregate(f"down{it}", pruned_base=(2 * it + 1) * NB)
                fold(5 + 3 * it, twice[:, 0:D]).then_inc(folded, 1)

                name = f"up{it}"
                pe.wait_ge(up_ready, it + 1)

                def turn(k, i, c, it=it):
                    o, w = HALF_CHUNKS[c]
                    if c == 0:
                        pe.wait_ge(col_ready, i * RING + (it * NB + k + 1))
                    pe.wait_ge(up_pruned, i * (4 * RING) + (4 * (it * NB + k) + c + 1))
                    for h in range(2):
                        for t in range(0, w, P):
                            last = mm(bank(4 + 2 * (c % 2) + h, P, t),
                                      sign_cols[k % 2][:, h * HALF + o + t:h * HALF + o + t + P], ident_b[:, :])
                    last.then_inc(signs_t, 1)

                def gather(k, i, c, it=it, name=name):
                    o, w = HALF_CHUNKS[c]
                    slot = slot_of(name, k)
                    pe.wait_ge(up_pruned, i * (4 * RING) + (4 * (it * NB + k) + c + 3))
                    if c == 0:
                        pe.wait_ge(stat_ready, i * RING + (stats_before[name] + k + 1))
                    for h in range(2):
                        last = mm(ps[h * D:(h + 1) * D, o:o + w], stat[:, k % 2 * D:(k % 2 + 1) * D],
                                  slot[:, h * HALF + o:h * HALF + o + w], start=k == 0)
                    if c == 3:
                        last.then_inc(block_done, 1)

                def up_step(k, i):
                    turn(k, i, 0)
                    if k > 0:
                        gather(k - 1, i, 3)
                    for c in range(1, 4):
                        turn(k, i, c)
                        gather(k, i, c - 1)
                each_block(pe, up_step)
                gather(NB % RING - 1 + RING, NB // RING - 1, 3)
                fold(6 + 3 * it, W["theta"]).then_inc(folded, 1)

        @block.scalar
        def _(act):
            def evac(n_done, e):
                act.wait_ge(block_done, RING + n_done)
                act.activation(agg_f[:, 0:2 * BANK], ps[:, 0:2 * BANK], ACT.Copy).then_inc(evac_act, 1)

            def features(r):
                act.wait_ge(xt_psum, r + 1)
                act.activation(xt[:, 0:2 * BANK], ps[:, 0:2 * BANK], ACT.Copy).then_inc(xt_act, 1)

            def root(dst, src, ready, n, done, bias=0.0):
                act.wait_ge(ready, n)
                act.activation(dst, src, ACT.Sqrt, bias=bias).then_inc(done, 1)

            lns = [0]

            def layernorm_root():
                lns[0] += 1
                root(small["var"][:, :], small["mean"][:, :], ln_var, lns[0], ln_sd, bias=eps_t[:, 0:1])

            act.wait_ge(consts_made, 5)
            evac(BASE["hop1"], 0)
            act.wait_ge(folded, 1)
            act.activation(by_half(cur[:, :])[:, :, :, :], node_psum(4), ACT.Tanh).then_inc(x_ready, 1)
            features(0)
            evac(BASE["ode"], 1)
            act.wait_ge(folded, 2)
            act.activation(by_half(scr_a), node_psum(4), ACT.Tanh).then_inc(tanh_done, 1)
            layernorm_root()
            evac(BASE["decay0"], 2)
            layernorm_root()
            features(1)
            for q in range(2):
                def relu(k, i, q=q):
                    act.wait_ge(decay_used, i * RING + (q * NB + k + 3))
                    for c, (o, w) in enumerate(QUART_CHUNKS):
                        act.wait_ge(tri_done, i * (4 * RING) + (4 * (q * NB + k) + 2 * c + 1))
                        dst = decay[k % 2].bitcast(I16)[:, o:o + w]
                        act.activation(dst, bank(c, w), ACT.Relu).then_inc(relu_act, 1)
                each_block(act, relu)
            act.wait_ge(decay_used, 4 + 2 * NB)
            act.activation(agg_f[:, 0:QUART], bank(4, QUART), ACT.Copy).then_inc(evac_act, 1)
            layernorm_root()

            def first_parts(n, stacks):
                act.wait_ge(cut_act, n)
                for dst, side in stacks:
                    last = act.activation(dst[side, :], part1[side, :], ACT.Copy)
                last.then_inc(stack_act, 1)

            for it in range(2):
                features(2 + it)
                act.wait_ge(parts, it + 1)
                for h in range(2):
                    act.wait_ge(query_half, 2 * it + h + 1)
                    act.activation(full[:, h * HALF:(h + 1) * HALF], bank(4 - 4 * h, HALF), ACT.Identity,
                                   bias=tiny["query_shift"][:, :], scale=D ** -0.5).then_inc(query_f32, 1)
                act.wait_ge(query_f32, 2 * it + 2)
                act.activation(part1, full, ACT.Copy).then_inc(cut_act, 1)
                first_parts(2 * it + 1, ((query12, LO), (query13, LO)))
                root(small["structural"][:, :], small["imp"][:, :], struct_sq, it + 1, struct_done)
                root(small["norm"][:, :], small["rnorm"][:, :], norm_sq, it + 1, norm_rt)
                evac(BASE[f"att{it}"], 4 + 3 * it)
                act.wait_ge(dup_psum, it + 1)
                act.wait_ge(cut_ready, 2 * it + 1)
                act.activation(two(part1), halves_psum(), ACT.Copy).then_inc(cut_act, 1)
                first_parts(2 * it + 2, ((right12, LO), (right21, HI), (right31, HI)))

                def exps(k, i, g):
                    act.wait_ge(negmax_ready, i * RING + (g * NB + k + 1))
                    act.activation(prod[k % 2][:, 0:N], prod[k % 2][:, 0:N], ACT.Exp, bias=negmax[:, k % 2:k % 2 + 1],
                                   accum_out=rowsum[:, k % 2:k % 2 + 1]).then_inc(exp_done, 1)
                each_block(act, lambda k, i: exps(k, i, 2 * it))

                def node_exp(r):
                    act.wait_ge(soft_bias, r + 1)
                    act.activation(small["node_e"][:, :], small["node_z"][:, :], ACT.Exp, bias=tiny["ngmax"][:, :],
                                   accum_out=tiny["psum_"][:, :]).then_inc(part_sum, 1)
                node_exp(2 * it)
                def place(dst, src):
                    return act.activation(dst, src, ACT.Copy)
                act.wait_ge(hat_parts, 3 * it + 1)
                place(stacked(hat21)[:, :, 1], stacked(hat12)[:, :, 0])
                place(stacked(hat31)[:, :, 1], stacked(hat12)[:, :, 0])
                act.wait_ge(hat_parts, 3 * it + 2)
                place(stacked(hat21)[:, :, 0], stacked(hat12)[:, :, 1]).then_inc(hat_stacked, 1)
                place(stacked(hat13)[:, :, 0], stacked(hat12)[:, :, 0])
                act.wait_ge(hat_parts, 3 * it + 3)
                place(stacked(hat13)[:, :, 1], stacked(hat31)[:, :, 0]).then_inc(hat_stacked, 1)
                for n, dst in ((2, right21[:, :]), (4, cos13)):
                    act.wait_ge(hat_psum, 4 * it + n)
                    place(dst, ps[:, 4 * BANK:8 * BANK].bitcast(BF16)[:, 0:NP]).then_inc(hat_act, 1)

                def exp_and_sign(k, i):
                    g = 2 * it + 1
                    exps(k, i, g)
                    act.wait_ge(negcut_ready, i * RING + (it * NB + k + 1))
                    at = i * (RING * NP) + k * NP
                    act.activation(signs[:, bass.ds(at, N)], prod[k % 2][:, 0:N], ACT.Sign,
                                   bias=negcut[:, k % 2:k % 2 + 1]).then_inc(product_free, 1)
                act.wait_ge(hat_psum, 4 * it + 4)
                each_block(act, exp_and_sign)
                node_exp(2 * it + 1)
                root(small["dv"][:, :], small["node_z"][:, :], deg_sq, it + 1, deg_rt)
                evac(BASE[f"up{it}"], 5 + 3 * it)

                act.wait_ge(down_ready, it + 1)

                def columns(k, i):
                    act.wait_ge(signs_t, i * (4 * RING) + (4 * (it * NB + k) + 4))
                    at = i * (RING * P) + k * P
                    dst = sign_cols[k % 2].rearrange("p (b n) -> p b n", b=NB)
                    act.activation(dst, signs3[:, :, bass.ds(at, P)], ACT.Copy).then_inc(col_ready, 1)
                each_block(act, columns)
                evac(BASE[f"up{it}"] + NB, 6 + 3 * it)
                if it == 1:
                    layernorm_root()

        @block.vector
        def _(dve):
            links = [0]

            def link(ins):
                links[0] += 1
                ins.then_inc(dve_chain, 1)
                dve.wait_ge(dve_chain, links[0])

            def evac(n_done, cols=HALF - 2 * BANK):
                dve.wait_ge(block_done, RING + n_done)
                dve.tensor_copy(agg_f[:, 2 * BANK:HALF], ps[:, 2 * BANK:HALF]).then_inc(evac_dve, 1)

            def features(r):
                dve.wait_ge(xt_psum, r + 1)
                dve.tensor_copy(xt[:, 2 * BANK:HALF], ps[:, 2 * BANK:HALF]).then_inc(xt_dve, 1)

            lns = [0]

            def layernorm():
                s, q = blocks3(scr_a), blocks3(scr_b)
                mean = small["mean"]
                link(dve.tensor_reduce(mean[:, :], s, axis=X, op=ALU.add))
                link(dve.tensor_scalar(mean[:, :], mean[:, :], 1.0 / D, None, ALU.mult))
                link(dve.tensor_tensor(s, s, per_node(mean[:, :]), ALU.subtract))
                link(dve.tensor_tensor(q, s, s, ALU.mult))
                link(dve.tensor_reduce(mean[:, :], q, axis=X, op=ALU.add))
                dve.tensor_scalar(mean[:, :], mean[:, :], 1.0 / D, None, ALU.mult).then_inc(ln_var, 1)
                lns[0] += 1
                dve.wait_ge(ln_sd, lns[0])
                link(dve.reciprocal(small["var"][:, :], small["var"][:, :]))
                return dve.tensor_tensor(blocks3(cur[:, :]), s, per_node(small["var"][:, :]), ALU.mult)

            dve.wait_ge(const_loaded, 7 * 16)
            dve.tensor_copy(ident_b[:, :], ident).then_inc(consts_cast, 1)
            dve.tensor_copy(tri, rest[:, 0:P]).then_inc(consts_cast, 1)
            dve.tensor_copy(rest_tri, rest[:, P:2 * P]).then_inc(consts_cast, 1)

            evac(BASE["hop1"])
            features(0)
            evac(BASE["ode"])
            dve.wait_ge(tanh_done, 1)
            link(dve.tensor_tensor(scr_a, scr_a, xw[:, :], ALU.add))
            layernorm().then_inc(x_ready, 1)

            evac(BASE["decay0"])
            dve.wait_ge(folded, 3)
            dve.wait_ge(x_ready, 2)
            link(dve.tensor_tensor(by_half(scr_b), node_psum(4), by_half(cur[:, :]), ALU.mult))
            link(dve.tensor_reduce(small["mean"][:, :], blocks3(scr_b), axis=X, op=ALU.add))
            link(dve.tensor_scalar(small["mean"][:, :], small["mean"][:, :], 0.01, None, ALU.mult))
            link(dve.tensor_scalar(scr_a, cur[:, :], -0.1, 1.0, ALU.mult, ALU.add))
            link(dve.tensor_tensor(blocks3(scr_a), blocks3(scr_a), per_node(small["mean"][:, :]), ALU.subtract))
            link(dve.tensor_tensor(scr_a, scr_a, cur[:, :], ALU.add))
            layernorm().then_inc(x_ready, 1)

            features(1)
            dve.wait_ge(support_psum, 1)
            sup = support3.rearrange("p (b c d) -> p b c d", c=3, d=D)
            link(dve.tensor_scalar(by_half(scr_a), node_psum(4), float(1 << DECAY_SHIFT), None, ALU.mult))
            link(dve.tensor_copy(sup[:, :, 0], blocks3(scr_a)))
            link(dve.tensor_tensor(blocks3(scr_a), blocks3(scr_a), sup[:, :, 0], ALU.subtract))
            link(dve.tensor_copy(sup[:, :, 1], blocks3(scr_a)))
            dve.tensor_tensor(sup[:, :, 2], blocks3(scr_a), sup[:, :, 1], ALU.subtract).then_inc(support_ready, 1)

            for q in range(2):
                def mask_of(k, i, q=q):
                    slot = landed(dve, f"decay{q}", k, i)
                    dve.wait_ge(decay_used, i * RING + (q * NB + k + 1))
                    dve.tensor_scalar(nbr[(2 * q + k) % 4], slot[:, 0:2 * QUART], 0.0, None, ALU.not_equal)\
                        .then_inc(block_done, 1)

                def relu(k, i, q=q):
                    for c, (o, w) in enumerate(QUART_CHUNKS):
                        dve.wait_ge(tri_done, i * (4 * RING) + (4 * (q * NB + k) + 2 * c + 2))
                        dst = decay[k % 2].bitcast(I16)[:, QUART + o:QUART + o + w]
                        dve.tensor_scalar(dst, bank(2 + c, w), 0.0, None, ALU.max).then_inc(relu_dve, 1)

                mask_of(0, 0)
                mask_of(1, 0)
                with dve.Fori(0, NB // RING) as i:
                    for k in range(RING):
                        dve.wait_ge(decay_used, i * RING + (q * NB + k + 3))
                        relu(k, i)
                        mask_of(k + 2, i)
                for k in (NB - 2, NB - 1):
                    dve.wait_ge(decay_used, q * NB + k + 3)
                    relu(k, 0)
            dve.wait_ge(decay_used, 4 + 2 * NB)
            dve.tensor_copy(agg_f[:, QUART:HALF], bank(6, QUART)).then_inc(evac_dve, 1)
            dve.wait_ge(folded, 4)
            link(dve.tensor_tensor(by_half(scr_a), node_psum(0), by_half(cur[:, :]), ALU.add))
            link(dve.tensor_tensor(by_half(scr_a), by_half(scr_a), per_feature4(decay_bias), ALU.add))
            link(layernorm())
            dve.tensor_scalar(cur[:, (NB - 1) * D:NB * D], cur[:, (NB - 1) * D:NB * D], real[:, NB - 1:NB], None,
                              ALU.mult).then_inc(x_ready, 1)

            def cut_parts(source, as_halves, stacks, n):
                dve.wait_ge(cut_act, n)
                shape = two if as_halves else (lambda t: t)
                link(dve.tensor_tensor(shape(rest), source, shape(part1), ALU.subtract))
                link(dve.tensor_copy(part2, rest))
                link(dve.tensor_tensor(part3, rest, part2, ALU.subtract))
                dve.wait_ge(stack_act, n)
                for dst, side, src in stacks:
                    last = dve.tensor_copy(dst[side, :], src[side, :])
                last.then_inc(cut_ready, 1)

            def product_piece(name, k, i, c):
                g = PRODUCTS.index(name)
                if c == 0:
                    landed(dve, name, k, i)
                    dve.wait_ge(product_free, i * RING + (g * NB + k + 1))
                o, w = PIECES[c]
                w = min(w, N - o)
                dve.wait_ge(piece_ready, i * (3 * RING) + ((g * NB + k) * 3 + c + 1))
                dve.memset(gates[:, 3 * (k % 2) + c:3 * (k % 2) + c + 1], 0.0)
                dve.tensor_tensor_reduce(out=prod[k % 2][:, o:o + w], in0=bank(3 * ((k + c) % 2), w),
                                         in1=slot_of(name, k)[:, o:o + w], scale=1.0, scalar=-3.0e38, op0=ALU.mult,
                                         op1=ALU.max, accum_out=max3[:, 3 * (k % 2) + c:3 * (k % 2) + c + 1])\
                    .then_inc(piece_read, 1)

            def product_max(name, k, i):
                g = PRODUCTS.index(name)
                dve.wait_ge(piece_read, i * (3 * RING) + ((g * NB + k) * 3 + 3 + 2))
                one = slice(k % 2, k % 2 + 1)
                red = dve.tensor_reduce(rowmax[:, one], max3[:, 3 * (k % 2):3 * (k % 2) + 3], axis=X, op=ALU.max)
                if name.startswith("att"):
                    red.then_inc(block_done, 1)
                    dve.wait_ge(block_done, i * RING + (BASE[name] + k + 1 + RING))
                else:
                    red.then_inc(rowmax_done, 1)
                    dve.wait_ge(rowmax_done, i * RING + (g // 2 * NB + k + 1))
                dve.tensor_scalar(negmax[:, one], rowmax[:, one], -1.0, None, ALU.mult).then_inc(negmax_ready, 1)

            def product_pass(name, after):
                for c in range(3):
                    product_piece(name, 0, 0, c)
                product_max(name, 0, 0)

                def block(k, i):
                    product_piece(name, k, i, 0)
                    product_piece(name, k, i, 1)
                    after(k - 1, i)
                    product_piece(name, k, i, 2)
                    product_max(name, k, i)
                block(1, 0)
                with dve.Fori(0, NB // RING) as i:
                    for k in range(2, 2 + RING):
                        block(k, i)
                after(NB - 1, 0)

            def column_sums(g, dst):
                dve.wait_ge(colsum_psum, g + 1)
                dve.tensor_copy(col_rows, ps[:, 6 * BANK:8 * BANK]).then_inc(colsum_sbuf, 1)
                dve.wait_ge(colsum_t, g + 1)
                for h, rows_, cols in ((0, (0, 4), 4), (1, (0, 2), 4), (1, (2, 3), 2)):
                    v = bank(h).rearrange("p (s r z) -> p r s z", r=4, z=32)[:, rows_[0]:rows_[1], 0:cols, 0]
                    at = 16 * h + 4 * rows_[0]
                    o = dst[:, at:at + (rows_[1] - rows_[0]) * cols].rearrange("p (r s) -> p r s", s=cols)
                    last = dve.tensor_copy(o, v)
                return last

            def node_softmax(r, threshold, dst):
                dve.tensor_reduce(tiny["pmax"][:, :], small["node_z"][:, :], axis=X, op=ALU.max).then_inc(part_max, 1)
                dve.wait_ge(all_max, r + 1)
                dve.tensor_scalar(tiny["ngmax"][:, :], tiny["gmax"][:, :], -1.0, None, ALU.mult).then_inc(soft_bias, 1)
                dve.wait_ge(all_sum, r + 1)
                link(dve.tensor_scalar(tiny["thr"][:, :], tiny["gsum"][:, :], threshold, None, ALU.mult))
                link(dve.tensor_scalar(dst, small["node_e"][:, :], tiny["thr"][:, :], None, ALU.is_ge))

            for it in range(2):
                th_comp, th_edge, th_node = thresholds(it)
                S = {n: t[:, :] for n, t in small.items()}
                features(2 + it)
                dve.tensor_scalar(tiny["query_shift"][:, :], query_bias, D ** -0.5, None, ALU.mult).then_inc(parts, 1)
                dve.wait_ge(value_psum, it + 1)
                dve.tensor_tensor(by_half(scr_a), node_psum(0), per_feature4(value_bias), ALU.add).then_inc(value_ready, 1)
                dve.wait_ge(proj_psum, it + 1)
                dve.tensor_copy(by_half(xw[:, :]), node_psum(4)).then_inc(proj_read, 1)
                dve.wait_ge(proj_read, it + 1)
                link(dve.tensor_tensor(scr_b, xw[:, :], xw[:, :], ALU.mult))
                link(dve.tensor_reduce(S["imp"], blocks3(scr_b), axis=X, op=ALU.add))
                dve.tensor_scalar(S["imp"], S["imp"], 1e-16, None, ALU.max).then_inc(struct_sq, 1)
                link(dve.tensor_tensor(scr_b, cur[:, :], cur[:, :], ALU.mult))
                link(dve.tensor_reduce(S["rnorm"], blocks3(scr_b), axis=X, op=ALU.add))
                dve.tensor_scalar(S["rnorm"], S["rnorm"], 1e-16, None, ALU.max).then_inc(norm_sq, 1)
                cut_parts(full, False, ((query12, HI, part2), (query13, HI, part3)), 2 * it + 1)
                dve.wait_ge(norm_rt, it + 1)
                link(dve.tensor_scalar(S["rnorm"], S["norm"], 1e-8, None, ALU.max))
                link(dve.reciprocal(S["rnorm"], S["rnorm"]))
                evac(BASE[f"att{it}"])
                dve.wait_ge(dup_psum, it + 1)
                cut_parts(halves_psum(), True, ((right12, HI, part2), (right21, LO, part2), (right31, LO, part3)),
                          2 * it + 2)

                def weigh(k, i):
                    dve.wait_ge(exp_done, i * RING + (2 * it * NB + k + 1))
                    dve.reciprocal(rowmax[:, k % 2:k % 2 + 1], rowsum[:, k % 2:k % 2 + 1]).then_inc(rz_done, 1)
                    dve.wait_ge(rz_done, i * RING + (it * NB + k + 1))
                    dve.tensor_scalar(rz32[:, k % 2 * 32:(k % 2 + 1) * 32], ones32[:, :], rowmax[:, k % 2:k % 2 + 1],
                                      real[:, bass.ds(i * RING + k, 1)], ALU.mult, ALU.mult).then_inc(rz_ready, 1)
                product_pass(f"att{it}", weigh)
                link(column_sums(2 * it, S["colsum"]))
                dve.wait_ge(struct_done, it + 1)
                link(dve.tensor_scalar(S["imp"], S["structural"], 0.5, None, ALU.mult))
                link(dve.scalar_tensor_tensor(out=S["imp"], in0=S["colsum"], scalar=0.5 / N, in1=S["imp"],
                                              op0=ALU.mult, op1=ALU.add))
                link(dve.tensor_tensor(S["imp"], S["imp"], real, ALU.mult))
                link(dve.tensor_tensor(S["node_z"], S["imp"], not_real, ALU.add))
                node_softmax(2 * it, th_comp, S["comp"])
                link(dve.tensor_scalar(S["blocked"], S["comp"], -HUGE, HUGE, ALU.mult, ALU.add))
                if it == 0:
                    dve.wait_ge(kept_read, 1)
                link(dve.tensor_tensor(S["rnorm"], S["rnorm"], S["comp"], ALU.mult))
                link(dve.tensor_tensor(blocks3(scr_a), blocks3(cur[:, :]), per_node(S["rnorm"]), ALU.mult))
                for n, (dst, part) in enumerate(((hat12, 0), (hat12, 1), (hat31, 0))):
                    here = stacked(dst)[:, :, part]
                    if n < 2:
                        dve.tensor_copy(here, blocks3(scr_a)).then_inc(hat_parts, 1)
                        dve.wait_ge(hat_parts, 3 * it + n + 1)
                        if n == 0:
                            link(dve.tensor_tensor(blocks3(scr_a), blocks3(scr_a), here, ALU.subtract))
                    else:
                        dve.tensor_tensor(here, blocks3(scr_a), stacked(hat12)[:, :, 1], ALU.subtract)\
                            .then_inc(hat_parts, 1)
                for n, dst in ((1, right12), (3, right31)):
                    dve.wait_ge(hat_psum, 4 * it + n)
                    dve.tensor_copy(dst[:, :], ps[:, 0:4 * BANK].bitcast(BF16)[:, 0:NP]).then_inc(hat_dve, 1)

                def prune(k, i):
                    dve.wait_ge(exp_done, i * RING + ((2 * it + 1) * NB + k + 1))
                    one = slice(k % 2, k % 2 + 1)
                    at = bass.ds(i * RING + k, 1)
                    dve.scalar_tensor_tensor(out=cut[:, one], in0=rowsum[:, one], scalar=th_edge,
                                             in1=S["blocked"][:, at], op0=ALU.mult, op1=ALU.add).then_inc(cut_done, 1)
                    dve.wait_ge(cut_done, i * RING + (it * NB + k + 1))
                    dve.tensor_scalar(negcut[:, one], cut[:, one], -1.0, None, ALU.mult).then_inc(negcut_ready, 1)
                    slot = slot_of(f"cos{it}", k)
                    dve.scalar_tensor_tensor(out=slot[:, 0:N], in0=prod[k % 2][:, 0:N], scalar=cut[:, one],
                                             in1=slot[:, 0:N], op0=ALU.is_ge, op1=ALU.mult,
                                             accum_out=S["conn"][:, at]).then_inc(pruned, 1)
                product_pass(f"cos{it}", prune)

                link(dve.memset(signs3[:, :, N:NP], 0))
                link(column_sums(2 * it + 1, S["edeg"]))
                link(dve.tensor_scalar(S["edeg"], S["edeg"], 1e-6, None, ALU.max))
                link(dve.reciprocal(S["edeg"], S["edeg"]))
                link(dve.tensor_tensor(S["imp"], S["conn"], S["norm"], ALU.mult))
                link(dve.tensor_tensor(S["imp"], S["imp"], real, ALU.mult))
                link(dve.tensor_tensor(S["node_z"], S["imp"], not_real, ALU.add))
                node_softmax(2 * it + 1, th_node, S["imp"])
                link(dve.scalar_tensor_tensor(out=S["imp"], in0=S["conn"], scalar=0.0, in1=S["imp"],
                                              op0=ALU.is_gt, op1=ALU.mult))
                link(dve.tensor_tensor(S["imp"], S["imp"], S["comp"], ALU.mult))
                dve.tensor_scalar(S["node_z"], S["conn"], 1e-6, None, ALU.max).then_inc(deg_sq, 1)
                dve.wait_ge(deg_rt, it + 1)
                link(dve.reciprocal(S["dv"], S["dv"]))
                link(dve.tensor_tensor(S["imp"], S["imp"], S["dv"], ALU.mult))
                dve.tensor_tensor(blocks3(cur[:, :]), blocks3(xw[:, :]), per_node(S["imp"]), ALU.mult)\
                    .then_inc(down_ready, 1)

                def down(k, i):
                    slot = landed(dve, f"down{it}", k, i)
                    at = i * (RING * NP) + k * NP
                    dve.scalar_tensor_tensor(out=slot[:, 0:N], in0=signs[:, bass.ds(at, N)], scalar=0.0,
                                             in1=slot[:, 0:N], op0=ALU.is_ge, op1=ALU.mult).then_inc(pruned, 1)
                each_block(dve, down)
                evac(BASE[f"up{it}"])
                dve.wait_ge(folded, 5 + 2 * it)
                dve.tensor_tensor(by_half(cur[:, :]), node_psum(4), per_node4(S["edeg"]), ALU.mult).then_inc(up_ready, 1)

                def up(k, i):
                    slot = landed(dve, f"up{it}", k, i)
                    v = slot[:, :].rearrange("p (h n) -> p h n", h=2)
                    for c, (o, w) in enumerate(HALF_CHUNKS):
                        dve.wait_ge(signs_t, i * (4 * RING) + (4 * (it * NB + k) + c + 9))
                        b = 4 + 2 * (c % 2)
                        s = ps[:, b * BANK:(b + 2) * BANK].rearrange("p (h n) -> p h n", h=2)[:, :, 0:w]
                        dve.scalar_tensor_tensor(out=v[:, :, o:o + w], in0=s, scalar=0.0, in1=v[:, :, o:o + w],
                                                 op0=ALU.is_ge, op1=ALU.mult).then_inc(up_pruned, 1)
                each_block(dve, up)
                evac(BASE[f"up{it}"] + NB)
                dve.wait_ge(folded, 6 + 2 * it)
                link(dve.tensor_tensor(by_half(scr_a), node_psum(4), per_node4(S["dv"]), ALU.mult))
                if it == 0:
                    dve.tensor_scalar(cur[:, :], scr_a, 0.0, None, ALU.max).then_inc(x_ready, 1)
                else:
                    dve.wait_ge(kept, 32)
                    link(dve.scalar_tensor_tensor(out=scr_a, in0=scr_a, scalar=0.0, in1=xw[:, :],
                                                  op0=ALU.max, op1=ALU.add))
                    layernorm().then_inc(out_ready, 1)


def kernel(x, adj, L0_gnn_W, L1_gnn_t, L2_gnn_weight, L2_gnn_bias, L3_gnn_W, L3_gnn_Theta, L3_gnn_Wq, L3_gnn_bq,
           L3_gnn_Wv, L3_gnn_bv):
    import concourse.bacc as bacc
    from concourse.bass_utils import run_bass_kernel_spmd

    def f(a):
        return np.asarray(a)

    def nodes(a):
        return np.ascontiguousarray(a.reshape(NB, P, -1).transpose(1, 0, 2).reshape(P, -1))

    x, adj = f(x), f(adj)
    xp = np.zeros((NP, D), np.float32)
    xp[:N] = x
    ap = np.zeros((NP, NP), np.float32)
    ap[:N, :N] = adj
    x_feat = np.ascontiguousarray(xp.T.reshape(D, 2, HALF).transpose(1, 0, 2).reshape(P, HALF))
    w0 = f(L0_gnn_W)
    mats = [w0[0, :D], w0[0, D:], w0[1, :D], w0[1, D:], f(L2_gnn_weight), f(L3_gnn_W), f(L3_gnn_Theta), f(L3_gnn_Wv),
            f(L3_gnn_Wq), f(L3_gnn_Wq)]
    weights = np.concatenate([np.concatenate([m, m], 0) for m in mats], 1)
    rows = np.concatenate([np.broadcast_to(f(b)[None], (P, D)) for b in (L2_gnn_bias, L3_gnn_bv)], 1)
    bq = np.concatenate([f(L3_gnn_bq)] * 2)[:, None]
    eye = np.eye(P, dtype=np.float32)
    twice = np.tile(np.eye(D, dtype=np.float32), (2, 2))
    real = np.ones((P, NB), np.float32)
    real[N - (NB - 1) * P:, NB - 1] = 0
    consts = np.concatenate([eye, twice, real, np.where(real > 0, 0, -HUGE).astype(np.float32)], 1)
    later = np.tri(P, P, -1, dtype=np.float32)
    tri = -P * later + MARK * eye
    decay_consts = np.concatenate([tri, -P - tri], 1)

    arrays = {"adj": ap, "adj_t": np.ascontiguousarray(ap.T), "x_nodes": nodes(xp), "x_feat": x_feat,
              "weights": weights, "rows": rows, "bq": bq, "consts": consts, "decay_consts": decay_consts}
    arrays = {n: np.ascontiguousarray(a) for n, a in arrays.items()}
    nc = bacc.Bacc("TRN2", target_bir_lowering=False, num_devices=1)
    args = [nc.dram_tensor(n, a.shape, F32, kind="ExternalInput").ap() for n, a in arrays.items()]
    kept = nc.dram_tensor("x_kept", (P, NB * D), F32, kind="Internal").ap()
    out = nc.dram_tensor("out", (P, NB, D), F32, kind="ExternalOutput").ap()
    build_program(nc, *args, kept, out)
    r = run_bass_kernel_spmd(nc, [arrays], core_ids=[0])
    got = r.results[0]["out"]
    return np.ascontiguousarray(got.transpose(1, 0, 2).reshape(NP, D)[:N])
```

```python
from contextlib import ExitStack

import concourse.bass as bass
import numpy as np
from concourse import mybir

F32 = mybir.dt.float32
BF16 = mybir.dt.bfloat16
I16 = mybir.dt.int16
I8 = mybir.dt.int8
ALU = mybir.AluOpType
ACT = mybir.ActivationFunctionType
X = mybir.AxisListType.X
RMAX = bass.bass_isa.ReduceOp.max
RADD = bass.bass_isa.ReduceOp.add

N = 3327
D = 64
P = 128
NB = (N + P - 1) // P
NP = NB * P
HALF = NP // 2
HB = NB // 2
RING = 4
EARLY_RING = 8
BANK = 512
HALF_CHUNKS = [(o, min(BANK, HALF - o)) for o in range(0, HALF, BANK)]
QUART = HALF // 2
QUART_CHUNKS = [(o, min(BANK, QUART - o)) for o in range(0, QUART, BANK)]
PIECE = NP // 4
PIECES = [(o, min(PIECE, NP - o)) for o in range(0, NP, PIECE)]
ROW_CHUNKS = [(3 * P * c, 3 * P) for c in range(6)] + [(18 * P, 4 * P), (22 * P, 4 * P)]
LO, HI = slice(0, D), slice(D, P)
LN_EPS = 1e-5
HUGE = 1e30
NEIGHBOURS = 100
DECAY_SHIFT = 27
MARK = 1 << 14
THETA0, THETA_MAX, LAM = 0.000244, 0.0003, 0.1
EARLY_WEIGHTS = ["w0_agg", "w0_self", "w1_agg", "w1_self", "decay_w"]
LATE_WEIGHTS = ["hyper_w", "theta", "value_w", "query_w"]

PASSES = [("hop0", NB), ("hop1", NB), ("ode", NB), ("decay0", NB), ("decay1", NB)]
for _it in range(2):
    PASSES += [(f"{s}{_it}", NB) for s in ("edge", "att", "cos", "down", "up")]
BASE = {}
_n = 0
for _name, _count in PASSES:
    BASE[_name] = _n
    _n += _count
EARLY = BASE["edge0"]
RESIDENT = {"hop1", "ode"}
DESCENDING = {"hop1"}
AGGS = ["hop0", "hop1", "ode", "decay", "edge0", "down0", "up0", "edge1", "down1", "up1"]
PRODUCTS = ["att0", "cos0", "att1", "cos1"]


def early_places():
    places, loads, order = {}, [0] * EARLY_RING, list(range(EARLY_RING))
    for name, _ in PASSES:
        if BASE[name] >= EARLY:
            return places
        places[name] = order, tuple(loads)
        for m in range(EARLY_RING if name in RESIDENT else 0, NB):
            loads[order[m % EARLY_RING]] += 1
        order = [order[m % EARLY_RING] for m in range(NB - EARLY_RING, NB)]
        if PASSES[[n for n, _ in PASSES].index(name) + 1][0] in RESIDENT:
            order.reverse()


EARLY_PLACES = early_places()


def steps_of(name):
    return 3 * RING if name.startswith("att") else RING


def piece_place(name, k, c):
    if name.startswith("att"):
        return (4 * k + c) % 3, 3
    return ((0, 2), (1, 2), (2, 5), (0, 3))[c] if k % 2 == 0 else ((1, 3), (2, 3), (0, 3), (1, 3))[c]


def thresholds(it):
    base = THETA0 + (1.0 - np.exp(-LAM * it)) * (THETA_MAX - THETA0)
    return float(base), float(min(base, 0.8)), float(min(base, 0.7))


def build_program(nc, adj, adj_t, x_nodes, x_feat, early_weights, late_weights, rows, bq, consts, decay_consts, x_kept, out):
    ctx = ExitStack()
    with ctx:
        def sb(name, cols, dt):
            return ctx.enter_context(nc.sbuf_tensor(name, [P, cols], dt))

        def sem(name):
            return ctx.enter_context(nc.semaphore(name))

        slots = [sb(f"slot{i}", NP, F32) for i in range(RING)]
        arena = sb("arena", NB * NP // 4, F32)
        signs = arena[:, :].bitcast(I8)
        signs3 = signs.rearrange("p (b n) -> p b n", b=NB)
        pairs = sb("pairs", 2 * NP, F32)
        prod = [pairs[:, i * NP:(i + 1) * NP] for i in range(2)]
        agg_f = pairs[:, 0:HALF]
        col_rows = pairs[:, HALF:HALF + 2 * BANK]
        xw = sb("xw", NB * D, F32)
        cur = sb("cur", NB * D, F32)
        right12 = sb("right12", NP, BF16)
        right21 = sb("right21", NP, BF16)
        right31 = sb("right31", NP, BF16)
        cos13 = cur[:, :].bitcast(BF16)

        off = [0]

        def work(words):
            a = arena[:, off[0]:off[0] + words]
            off[0] += words
            return a
        xt = work(HALF)
        scr_a = work(NB * D)
        scr_b = work(NB * D)
        full = work(NP)
        rest = work(NP)
        part1 = work(NP // 2).bitcast(BF16)
        part2 = work(NP // 2).bitcast(BF16)
        part3 = work(NP // 2).bitcast(BF16)
        query12 = work(NP // 2).bitcast(BF16)
        query13 = work(NP // 2).bitcast(BF16)
        assert off[0] <= NB * NP // 4
        early_slots = slots + [arena[:, NB * NP // 4 - i * NP:NB * NP // 4 - (i - 1) * NP]
                               for i in range(1, EARLY_RING - RING + 1)]
        hat12, hat21 = (full[:, i * NP // 2:(i + 1) * NP // 2].bitcast(BF16) for i in range(2))
        hat31, hat13 = (rest[:, i * NP // 2:(i + 1) * NP // 2].bitcast(BF16) for i in range(2))
        diagonals = part1
        mask_row = part2
        support3 = full.bitcast(BF16)[:, 0:NB * 3 * D]
        nbr = [pairs[:, HALF + i * QUART:HALF + (i + 1) * QUART].bitcast(BF16) for i in range(4)]
        decay = [pairs[:, HALF + (4 + i) * QUART:HALF + (5 + i) * QUART] for i in range(2)]
        tri = right31[:, 0:P]
        rest_tri = right31[:, P:2 * P]
        start_bits = right31[:, 2 * P:3 * P]
        stat3 = [right31[:, (3 + 2 * i) * P:(3 + 2 * i) * P + 3 * D] for i in range(2)]
        sign_cols = [right12[:, :], right21[:, :]]

        wt = sb("wt", len(LATE_WEIGHTS) * P, F32)
        early_wt = right12[:, :].bitcast(F32)[:, 0:len(EARLY_WEIGHTS) * P]
        W = {n: t[:, i * P:(i + 1) * P] for names, t in ((EARLY_WEIGHTS, early_wt), (LATE_WEIGHTS, wt))
             for i, n in enumerate(names)}
        rowt = sb("rowt", 2 * D + 1, F32)
        decay_bias, value_bias, query_bias = rowt[:, 0:D], rowt[:, D:2 * D], rowt[:, 2 * D:2 * D + 1]
        cst = sb("cst", 2 * P + 2 * NB, F32)
        ident, twice = cst[:, 0:P], cst[:, P:2 * P]
        real, not_real = cst[:, 2 * P:2 * P + NB], cst[:, 2 * P + NB:2 * P + 2 * NB]
        ident_b = sb("ident_b", P, BF16)
        zeros_b = sb("zeros_b", P, BF16)
        ones_b = sb("ones_b", BANK, BF16)
        ones32 = sb("ones32", 32, F32)
        stat = sb("stat", 2 * D, F32)
        rz32 = sb("rz32", 2 * 32, F32)
        small = {n: sb(n, NB, F32) for n in
                 ("mean", "var", "structural", "colsum", "imp", "comp", "blocked", "norm", "rnorm",
                  "conn", "node_z", "node_e", "dv", "edeg")}
        tiny = {n: sb(n, 1, F32) for n in ("pmax", "gmax", "ngmax", "psum_", "gsum", "thr", "query_shift")}
        max4 = sb("max4", 2 * 4, F32)
        row_rz = sb("row_rz", 2, F32)
        gates = sb("gates", 10, F32)
        negmax = sb("negmax", 2, F32)
        rowsum = sb("rowsum", 2, F32)
        cut = sb("cut", 2, F32)
        eps_t = sb("eps_t", 1, F32)

        ps = ctx.enter_context(nc.psum_tensor("ps", [P, 8 * BANK], F32))

        def bank(b, cols=BANK, at=0):
            return ps[:, b * BANK + at:b * BANK + at + cols]

        def by_half(t):
            return t.rearrange("p (h b d) -> p h b d", h=2, d=D)

        def node_psum(first):
            return ps[:, first * BANK:first * BANK + NB * D].rearrange("p (b h d) -> p h b d", h=2, d=D)

        def halves_psum():
            return ps[:, :].rearrange("p (h n) -> p h n", h=2)[:, :, 0:HALF]

        def two(t):
            return t.rearrange("p (h n) -> p h n", h=2)

        def per_node(t):
            return t.unsqueeze(2).to_broadcast([P, NB, D])

        def per_node4(t):
            return t.rearrange("p (h b) -> p h b", h=2).unsqueeze(3).to_broadcast([P, 2, HB, D])

        def per_feature4(t):
            return t.unsqueeze(1).unsqueeze(1).to_broadcast([P, 2, HB, D])

        def stacked(t):
            return t.rearrange("p (b c d) -> p b c d", c=2, d=D)

        def blocks3(t):
            return t.rearrange("p (b d) -> p b d", d=D)

        slot_loaded = [sem(f"slot_loaded{i}") for i in range(RING)]
        early_loaded = [sem(f"early_loaded{i}") for i in range(EARLY_RING)]
        block_done = sem("block_done")
        stat_ready = sem("stat_ready")
        const_loaded = sem("const_loaded")
        consts_made = sem("consts_made")
        consts_cast = sem("consts_cast")
        evac_act = sem("evac_act")
        evac_dve = sem("evac_dve")
        folded = sem("folded")
        x_ready = sem("x_ready")
        xt_psum = sem("xt_psum")
        xt_act = sem("xt_act")
        xt_dve = sem("xt_dve")
        dve_chain = sem("dve_chain")
        centred = sem("centred")
        squared = sem("squared")
        ln_var = sem("ln_var")
        ln_sd = sem("ln_sd")
        tanh_done = sem("tanh_done")
        biased = sem("biased")
        support_psum = sem("support_psum")
        support_ready = sem("support_ready")
        tri_done = sem("tri_done")
        relu_act = sem("relu_act")
        relu_dve = sem("relu_dve")
        decay_used = sem("decay_used")
        kept = sem("kept")
        kept_read = sem("kept_read")
        proj_psum = sem("proj_psum")
        proj_read = sem("proj_read")
        struct_sq = sem("struct_sq")
        struct_done = sem("struct_done")
        query_f32 = sem("query_f32")
        parts = sem("parts")
        cut_act = sem("cut_act")
        stack_act = sem("stack_act")
        cut_ready = sem("cut_ready")
        pool_chain = sem("pool_chain")
        hat_parts = sem("hat_parts")
        turned = sem("turned")
        turned_dve = sem("turned_dve")
        turned_act = sem("turned_act")
        diagonal_ready = sem("diagonal_ready")
        mask_psum = sem("mask_psum")
        mask_ready = sem("mask_ready")
        right_ready = sem("right_ready")
        query_half = sem("query_half")
        value_psum = sem("value_psum")
        dup_psum = sem("dup_psum")
        piece_ready = sem("piece_ready")
        piece_read = sem("piece_read")
        negmax_ready = sem("negmax_ready")
        exp_done = sem("exp_done")
        rz_done = sem("rz_done")
        rz_ready = sem("rz_ready")
        row_cut = sem("row_cut")
        pruned = sem("pruned")
        product_free = sem("product_free")
        colsum_psum = sem("colsum_psum")
        colsum_sbuf = sem("colsum_sbuf")
        colsum_t = sem("colsum_t")
        part_max = sem("part_max")
        all_max = sem("all_max")
        part_sum = sem("part_sum")
        all_sum = sem("all_sum")
        soft_bias = sem("soft_bias")
        norm_sq = sem("norm_sq")
        norm_rt = sem("norm_rt")
        deg_sq = sem("deg_sq")
        deg_rt = sem("deg_rt")
        down_ready = sem("down_ready")
        up_ready = sem("up_ready")
        value_ready = sem("value_ready")
        col_ready = sem("col_ready")
        signs_t = sem("signs_t")
        up_pruned = sem("up_pruned")
        out_ready = sem("out_ready")
        stored = sem("stored")

        block = ctx.enter_context(nc.Block())

        def ring_of(name):
            return EARLY_RING if BASE[name] < EARLY else RING

        def each_block(eng, body, ring=RING):
            head = NB % ring
            for k in range(head):
                body(k, 0)
            with eng.Fori(0, NB // ring) as i:
                for k in range(head, head + ring):
                    body(k, i)

        def place_of(name, k):
            if BASE[name] < EARLY:
                order, loads = EARLY_PLACES[name]
                s = order[k % EARLY_RING]
                return early_slots[s], early_loaded[s], loads[s] + k // EARLY_RING + (name not in RESIDENT)
            n = BASE[name] + k - EARLY
            return slots[n % RING], slot_loaded[n % RING], n // RING + 1

        def landed(eng, name, k, i):
            slot, loaded, loads = place_of(name, k)
            eng.wait_ge(loaded, (loads + i) * 16)
            return slot

        def slot_of(name, k):
            return place_of(name, k)[0]

        @block.sync
        def _(sp):
            sp.dma_start(xw[:, :], x_nodes).then_inc(const_loaded, 16)
            sp.dma_start(xt, x_feat).then_inc(const_loaded, 16)
            sp.dma_start(cst[:, :], consts).then_inc(const_loaded, 16)
            sp.dma_start(early_wt, early_weights).then_inc(const_loaded, 16)
            sp.dma_start(wt[:, :], late_weights).then_inc(const_loaded, 16)
            sp.dma_start(rowt[:, 0:2 * D], rows).then_inc(const_loaded, 16)
            sp.dma_start(rowt[:, 2 * D:2 * D + 1], bq).then_inc(const_loaded, 16)
            sp.dma_start(full[:, 0:2 * P], decay_consts).then_inc(const_loaded, 16)

            def stream(name, source, quarter=None):
                ring = ring_of(name)
                down_rows = quarter is not None or name in DESCENDING

                def load(k, i):
                    n = BASE[name] + k
                    row = i * (-ring * P) + (NB - 1 - k) * P if down_rows else i * (ring * P) + k * P
                    row = row if isinstance(row, int) else sp.snap(row)
                    used = n + 1 + EARLY_RING - ring
                    sp.wait_ge(block_done, EARLY_RING + EARLY if name == "edge0" and k < 2 else i * ring + used)
                    slot, loaded, _ = place_of(name, k)
                    if quarter is None:
                        src, dst = source[bass.ds(row, P), :], slot[:, :]
                    else:
                        src = source[bass.ds(row, P), :].rearrange("p (h n) -> p h n", h=2)
                        src = src[:, :, quarter * QUART:(quarter + 1) * QUART]
                        dst = slot[:, 0:2 * QUART].rearrange("p (h n) -> p h n", h=2)
                    sp.dma_start(dst, src).then_inc(loaded, 16)
                if name not in RESIDENT:
                    each_block(sp, load, ring)
                    return
                head = NB % ring
                for k in range(head):
                    load(ring + k, 0)
                with sp.Fori(0, NB // ring - 1) as i:
                    for k in range(head, head + ring):
                        load(ring + k, i)

            stream("hop0", adj_t)
            stream("hop1", adj_t)
            stream("ode", adj_t)
            stream("decay0", adj_t, 0)
            stream("decay1", adj_t, 1)
            for it in range(2):
                stream(f"edge{it}", adj)
                if it == 0:
                    sp.wait_ge(x_ready, 4)
                    sp.dma_start(x_kept, cur[:, :]).then_inc(kept, 16)
                    sp.wait_ge(kept, 16)
                    sp.sem_inc(kept_read, 1)
                stream(f"att{it}", adj)
                stream(f"cos{it}", adj)
                stream(f"down{it}", adj)
                if it == 1:
                    sp.wait_ge(down_ready, 2)
                    sp.dma_start(xw[:, :], x_kept).then_inc(kept, 16)
                stream(f"up{it}", adj_t)
            sp.wait_ge(out_ready, 1)
            sp.dma_start(out, blocks3(cur[:, :])[:, :, :]).then_inc(stored, 16)
            sp.wait_ge(stored, 16)

        @block.gpsimd
        def _(pool):
            pool.memset(zeros_b[:, :], 0.0).then_inc(consts_made, 1)
            pool.memset(ones_b[:, :], 1.0).then_inc(consts_made, 1)
            pool.memset(ones32[:, :], 1.0).then_inc(consts_made, 1)
            pool.memset(start_bits, -float(MARK - NEIGHBOURS * P) / P).then_inc(consts_made, 1)
            pool.memset(eps_t[:, :], LN_EPS).then_inc(consts_made, 1)

            steps = [0]

            def linked(ins):
                steps[0] += 1
                ins.then_inc(pool_chain, 1)
                pool.wait_ge(pool_chain, steps[0])

            def feed(name, source):
                ring = ring_of(name)

                def copy(k, i):
                    pool.wait_ge(block_done, i * ring + (BASE[name] + k + EARLY_RING - 1))
                    at = i * (-ring * D) + (NB - 1 - k) * D if name in DESCENDING else i * (ring * D) + k * D
                    pool.tensor_copy(stat[:, k % 2 * D:(k % 2 + 1) * D], source[:, bass.ds(at, D)])\
                        .then_inc(stat_ready, 1)
                each_block(pool, copy, ring)

            def feed_decay(q):
                def copy(k, i):
                    pool.wait_ge(decay_used, i * EARLY_RING + (q * NB + k + 3))
                    at = i * (-EARLY_RING * 3 * D) + (NB - 1 - k) * 3 * D
                    pool.tensor_copy(stat3[k % 2], support3[:, bass.ds(at, 3 * D)]).then_inc(stat_ready, 1)
                each_block(pool, copy, EARLY_RING)

            def node_softmax(r):
                pool.wait_ge(part_max, r + 1)
                pool.partition_all_reduce(tiny["gmax"][:, :], tiny["pmax"][:, :], P, RMAX).then_inc(all_max, 1)
                pool.wait_ge(part_sum, r + 1)
                pool.partition_all_reduce(tiny["gsum"][:, :], tiny["psum_"][:, :], P, RADD).then_inc(all_sum, 1)

            pool.wait_ge(const_loaded, 8 * 16)
            feed("hop0", xw)
            pool.wait_ge(x_ready, 1)
            feed("hop1", cur)
            pool.wait_ge(x_ready, 2)
            feed("ode", cur)
            pool.wait_ge(x_ready, 3)
            pool.tensor_tensor(blocks3(scr_b), blocks3(cur[:, :]), decay_bias.unsqueeze(1).to_broadcast([P, NB, D]),
                               ALU.add).then_inc(biased, 1)
            pool.wait_ge(support_ready, 1)
            feed_decay(0)
            feed_decay(1)
            for it in range(2):
                pool.wait_ge(value_ready, it + 1)
                feed(f"edge{it}", scr_a)
                pool.wait_ge(cut_ready, 2 * it + 2)
                hat = blocks3(scr_a)
                p1, p2, p3 = stacked(hat12)[:, :, 0], stacked(hat12)[:, :, 1], stacked(hat31)[:, :, 0]
                linked(pool.tensor_tensor(hat, blocks3(cur[:, :]), per_node(small["rnorm"][:, :]), ALU.mult))
                linked(pool.tensor_copy(p1, hat))
                linked(pool.tensor_tensor(hat, hat, p1, ALU.subtract))
                linked(pool.tensor_copy(p2, hat))
                linked(pool.tensor_tensor(p3, hat, p2, ALU.subtract))
                for dst, part, src in ((hat21, 0, p2), (hat21, 1, p1), (hat31, 1, p1), (hat13, 0, p1), (hat13, 1, p3)):
                    last = pool.tensor_copy(stacked(dst)[:, :, part], src)
                last.then_inc(hat_parts, 1)
                node_softmax(2 * it)
                node_softmax(2 * it + 1)
                pool.wait_ge(down_ready, it + 1)
                feed(f"down{it}", cur)
                pool.wait_ge(up_ready, it + 1)
                feed(f"up{it}", cur)

        @block.tensor
        def _(pe):
            pe.sem_inc(block_done, EARLY_RING)
            pe.sem_inc(piece_read, 5)
            pe.sem_inc(product_free, 2)
            pe.sem_inc(decay_used, 4)
            pe.sem_inc(signs_t, 8)
            pe.sem_inc(up_pruned, 2)
            pe.wait_ge(const_loaded, 8 * 16)
            pe.wait_ge(consts_made, 5)
            pe.wait_ge(consts_cast, 3)

            stats_before = {n: sum(2 * NB if a == "decay" else NB for a in AGGS[:AGGS.index(n)]) for n in AGGS}

            def mm(o, l, r, start=True, stop=True):
                return pe.matmul(o, l, r, start=start, stop=stop, skip_group_check=True)

            def aggregate(name, pruned_base=None, between=None):
                ring = ring_of(name)

                def step(k, i):
                    if pruned_base is None:
                        slot = landed(pe, name, k, i)
                    else:
                        slot = slot_of(name, k)
                        pe.wait_ge(pruned, i * ring + (pruned_base + k + 1))
                    pe.wait_ge(stat_ready, i * ring + (stats_before[name] + k + 1))
                    s = stat[:, k % 2 * D:(k % 2 + 1) * D]
                    for o, w in HALF_CHUNKS:
                        for h in range(2):
                            last = mm(ps[h * D:(h + 1) * D, o:o + w], s, slot[:, h * HALF + o:h * HALF + o + w],
                                      start=k == 0)
                    last.then_inc(block_done, 1)
                if between is None:
                    each_block(pe, step, ring)
                    return
                first = 10
                for k in range(first):
                    step(k, 0)
                    between(k)
                with pe.Fori(0, (NB - first) // ring) as i:
                    for k in range(first, first + ring):
                        step(k, i)

            def fold(e, right, first=4, also=None):
                pe.wait_ge(evac_act, e + 1)
                pe.wait_ge(evac_dve, e + 1)
                return to_nodes(agg_f, right, first, also)

            def to_nodes(left, right, first, also=None):
                for b in range(HB):
                    o = ps[:, first * BANK + b * P:first * BANK + (b + 1) * P]
                    last = mm(o, left[:, b * P:(b + 1) * P], right, stop=also is None)
                    if also is not None:
                        last = mm(o, xt[:, b * P:(b + 1) * P], also, start=False)
                return last

            def to_features(source, first):
                for b in range(HB):
                    for h in range(2):
                        last = mm(ps[h * D:(h + 1) * D, first * BANK + b * P:first * BANK + (b + 1) * P],
                                  source[:, (h * HB + b) * D:(h * HB + b + 1) * D], ident)
                return last

            def on_both_partition_halves(left, right, h, first):
                for o, w in HALF_CHUNKS:
                    last = mm(bank(first, w, o), left[h * D:(h + 1) * D, :], right[h * D:(h + 1) * D, o:o + w])
                return last

            def to_stack(source, half, first):
                dst = ps[:, first * BANK:(first + 2) * BANK].bitcast(BF16)
                for b in range(HB):
                    at = (half * HB + b) * P
                    last = pe.transpose(dst[:, b * P:(b + 1) * P], source[:, at:at + P], ident_b[:, :])
                last.then_inc(turned, 1)

            def features_round(r):
                pe.wait_ge(x_ready, r)
                to_features(cur[:, :], 0).then_inc(xt_psum, 1)

            aggregate("hop0")
            fold(0, W["w0_agg"], also=W["w0_self"]).then_inc(folded, 1)
            features_round(1)
            pe.wait_ge(xt_act, 1)
            pe.wait_ge(xt_dve, 1)
            aggregate("hop1")
            fold(1, W["w1_agg"], also=W["w1_self"]).then_inc(folded, 1)
            aggregate("ode")
            fold(2, ident).then_inc(folded, 1)
            features_round(3)
            pe.wait_ge(xt_act, 2)
            pe.wait_ge(xt_dve, 2)
            to_nodes(xt, W["decay_w"], 4).then_inc(support_psum, 1)
            for q in range(2):
                if q:
                    pe.wait_ge(relu_act, 2 * NB)
                    pe.wait_ge(relu_dve, 2 * NB)
                for b in range(4):
                    mm(bank(b), start_bits, ones_b[:, :])

                def marks(k):
                    return nbr[(2 * q + k) % 4]

                def own_bits(k, i, c, q=q, marks=marks):
                    if c == 0:
                        pe.wait_ge(block_done, i * EARLY_RING + (BASE[f"decay{q}"] + k + 1 + EARLY_RING))
                    o, w = QUART_CHUNKS[c]
                    for s in range(2):
                        mm(bank(2 * s + c, w), tri, marks(k)[:, s * QUART + o:s * QUART + o + w], start=False)\
                            .then_inc(tri_done, 1)

                def step(k, i, last_block=False, q=q, marks=marks, own_bits=own_bits):
                    dw = decay[k % 2].bitcast(BF16)
                    for c, (o, w) in enumerate(QUART_CHUNKS):
                        pe.wait_ge(relu_act, i * (2 * EARLY_RING) + (2 * (q * NB + k) + c + 1))
                        pe.wait_ge(relu_dve, i * (2 * EARLY_RING) + (2 * (q * NB + k) + c + 1))
                        if not last_block:
                            for s in range(2):
                                mm(bank(2 * s + c, w), rest_tri, marks(k)[:, s * QUART + o:s * QUART + o + w],
                                   start=False)
                            own_bits(k + 1, i, c)
                        if c == 0:
                            pe.wait_ge(stat_ready, i * EARLY_RING + (stats_before["decay"] + q * NB + k + 1))
                        for part in range(3):
                            for s in range(2):
                                last = mm(ps[s * D:(s + 1) * D, (4 + 2 * q + c) * BANK:(4 + 2 * q + c) * BANK + w],
                                          stat3[k % 2][:, part * D:(part + 1) * D],
                                          dw[:, s * QUART + o:s * QUART + o + w], start=False)
                    last.then_inc(decay_used, 1)

                for c in range(2):
                    own_bits(0, 0, c)
                if q == 0:
                    pe.wait_ge(support_ready, 1)
                for b in (4 + 2 * q, 5 + 2 * q):
                    mm(bank(b), zeros_b[:, :], ones_b[:, :])
                with pe.Fori(0, NB // EARLY_RING) as i:
                    for k in range(EARLY_RING):
                        step(k, i)
                step(NB - 2, 0)
                step(NB - 1, 0, last_block=True)
            fold(3, ident, first=0).then_inc(folded, 1)

            def product(name, left12, left13, before_sums=None, after_sums=None):
                it = PRODUCTS.index(name) // 2
                steps = steps_of(name)
                g = PRODUCTS.index(name)
                sums = name.startswith("att")
                for b in (6, 7):
                    mm(bank(b), zeros_b[:, :], ones_b[:, :])

                def piece(k, i, c):
                    at = i * (steps * P) + k * P
                    o, w = PIECES[c]
                    buf, ago = piece_place(name, k, c)
                    if not sums and k == 0:
                        pe.wait_ge(right_ready, 2 * it + c // 2 + 1)
                    pe.wait_ge(piece_read, i * (steps * 4) + ((g * NB + k) * 4 + c + 1 - ago + 5))
                    for n, (left, right) in enumerate(((left12, right12), (left12, right21), (left13, right31))):
                        for s in range(0, w, BANK):
                            v = min(BANK, w - s)
                            last = mm(bank(2 * buf, v, s), left[:, bass.ds(at, P)], right[:, o + s:o + s + v],
                                      start=n == 0)
                    last.then_inc(piece_ready, 1)

                def columns(k, i):
                    if sums:
                        pe.wait_ge(rz_ready, i * steps + (g // 2 * NB + k + 1))
                        moving, s = prod[k % 2], rz32[:, k % 2 * 32:(k % 2 + 1) * 32]
                    else:
                        pe.wait_ge(pruned, i * RING + (g // 2 * 2 * NB + k + 1))
                        moving, s = slot_of(name, k), ones32[:, :]
                    for c, (o, w) in enumerate(ROW_CHUNKS):
                        r = c % 4
                        w = min(w, N - o)
                        last = mm(ps[32 * r:32 * r + 32, (6 + c // 4) * BANK:(6 + c // 4) * BANK + w], s,
                                  moving[:, o:o + w], start=False)
                    last.then_inc(product_free if sums else block_done, 1)
                    return last

                for k in range(2):
                    for c in range(4):
                        piece(k, 0, c)
                if sums:
                    with pe.Fori(0, NB // steps) as i:
                        for k in range(2, 2 + steps):
                            piece(k, i, 0)
                            columns(k - 2, i)
                            piece(k, i, 1)
                            piece(k, i, 2)
                            piece(k, i, 3)
                else:
                    def block(k, i, last_block=False):
                        piece(k, i, 3)
                        if not last_block:
                            piece(k + 1, i, 0)
                            piece(k + 1, i, 1)
                        columns(k - 2, i)
                        if not last_block:
                            piece(k + 1, i, 2)
                    for c in range(3):
                        piece(2, 0, c)
                    with pe.Fori(0, NB // RING - 1) as i:
                        for k in range(2, 2 + RING):
                            block(k, i)
                    for k in range(NB - RING, NB):
                        block(k, 0, last_block=k == NB - 1)
                columns(NB - 2, 0)
                if before_sums is not None:
                    pe.wait_ge(piece_read, (g + 1) * NB * 4 + 5)
                    before_sums()
                columns(NB - 1, 0)
                mm(bank(5, 1), zeros_b[:, :], ones_b[:, 0:1]).then_inc(colsum_psum, 1)
                if after_sums is not None:
                    after_sums()
                pe.wait_ge(colsum_sbuf, g + 1)
                for t in range(8):
                    last = pe.transpose(ps[:, 6 * BANK + t * P:6 * BANK + (t + 1) * P], col_rows[:, t * P:(t + 1) * P],
                                        ident)
                last.then_inc(colsum_t, 1)

            for it in range(2):
                features_round(4 + it)
                pe.wait_ge(xt_act, 3 + it)
                pe.wait_ge(xt_dve, 3 + it)
                to_nodes(xt, W["value_w"], 0).then_inc(value_psum, 1)
                pe.wait_ge(value_ready, it + 1)

                def between(k, it=it):
                    if k == 1:
                        on_both_partition_halves(W["query_w"], xt, 0, 4).then_inc(query_half, 1)
                    elif k == 5:
                        pe.wait_ge(query_f32, 2 * it + 1)
                        on_both_partition_halves(W["query_w"], xt, 1, 4).then_inc(query_half, 1)
                    elif k == 9:
                        pe.wait_ge(query_f32, 2 * it + 2)
                        to_nodes(xt, W["hyper_w"], 4).then_inc(proj_psum, 1)
                aggregate(f"edge{it}", between=between)
                pe.wait_ge(evac_act, 5 + 3 * it)
                pe.wait_ge(evac_dve, 5 + 3 * it)
                pe.wait_ge(proj_read, it + 1)
                for h in range(2):
                    last = on_both_partition_halves(twice, agg_f, h, 4 * h)
                last.then_inc(dup_psum, 1)
                pe.wait_ge(cut_ready, 2 * it + 2)

                def first_stack(it=it):
                    pe.wait_ge(hat_parts, it + 1)
                    to_stack(hat12, 0, 0)
                    to_stack(hat12, 1, 2)

                def second_stack(it=it):
                    to_stack(hat21, 0, 4)
                    pe.wait_ge(turned_dve, 4 * it + 1)
                    to_stack(hat21, 1, 0)
                product(f"att{it}", query12, query13, first_stack, second_stack)
                pe.wait_ge(turned_dve, 4 * it + 2)
                to_stack(hat31, 0, 2)
                pe.wait_ge(turned_act, 4 * it + 1)
                to_stack(hat31, 1, 4)
                pe.wait_ge(turned_act, 4 * it + 2)
                to_stack(hat13, 0, 0)
                pe.wait_ge(turned_act, 4 * it + 3)
                to_stack(hat13, 1, 2)
                for h, (first, taken, n) in enumerate(((4, turned_act, 4), (0, turned_dve, 4))):
                    pe.wait_ge(diagonal_ready, 2 * it + h + 1)
                    pe.wait_ge(taken, 4 * it + n)
                    for o, w in HALF_CHUNKS:
                        last = mm(bank(first, w, o), ones_b[:, 0:P], diagonals[:, h * HALF + o:h * HALF + o + w])
                    last.then_inc(mask_psum, 1)
                pe.wait_ge(mask_ready, 2 * it + 2)
                product(f"cos{it}", right12, cos13)
                aggregate(f"down{it}", pruned_base=(2 * it + 1) * NB)
                fold(5 + 3 * it, ident).then_inc(folded, 1)

                name = f"up{it}"
                pe.wait_ge(up_ready, it + 1)

                def turn(k, i, c, it=it):
                    o, w = HALF_CHUNKS[c]
                    if c == 0:
                        pe.wait_ge(col_ready, i * RING + (it * NB + k + 1))
                    pe.wait_ge(up_pruned, i * (4 * RING) + (4 * (it * NB + k) + c + 1))
                    for h in range(2):
                        for t in range(0, w, P):
                            last = mm(bank(4 + 2 * (c % 2) + h, P, t),
                                      sign_cols[k % 2][:, h * HALF + o + t:h * HALF + o + t + P], ident_b[:, :])
                    last.then_inc(signs_t, 1)

                def gather(k, i, c, it=it, name=name):
                    o, w = HALF_CHUNKS[c]
                    slot = slot_of(name, k)
                    pe.wait_ge(up_pruned, i * (4 * RING) + (4 * (it * NB + k) + c + 3))
                    if c == 0:
                        pe.wait_ge(stat_ready, i * RING + (stats_before[name] + k + 1))
                    for h in range(2):
                        last = mm(ps[h * D:(h + 1) * D, o:o + w], stat[:, k % 2 * D:(k % 2 + 1) * D],
                                  slot[:, h * HALF + o:h * HALF + o + w], start=k == 0)
                    if c == 3:
                        last.then_inc(block_done, 1)

                def up_step(k, i):
                    for c in range(4):
                        turn(k, i, c)
                        if c >= 2:
                            gather(k, i, c - 2)
                        elif k > 0:
                            gather(k - 1, i, c + 2)
                each_block(pe, up_step)
                gather(NB - 1, 0, 2)
                gather(NB - 1, 0, 3)
                fold(6 + 3 * it, W["theta"]).then_inc(folded, 1)

        @block.scalar
        def _(act):
            def evac(n_done, e):
                act.wait_ge(block_done, EARLY_RING + n_done)
                act.activation(agg_f[:, 0:2 * BANK], ps[:, 0:2 * BANK], ACT.Copy).then_inc(evac_act, 1)

            def features(r):
                act.wait_ge(xt_psum, r + 1)
                act.activation(xt[:, 0:2 * BANK], ps[:, 0:2 * BANK], ACT.Copy).then_inc(xt_act, 1)

            def root(dst, src, ready, n, done, bias=0.0):
                act.wait_ge(ready, n)
                act.activation(dst, src, ACT.Sqrt, bias=bias).then_inc(done, 1)

            lns = [0]

            def layernorm_root():
                for h in range(2):
                    act.wait_ge(centred, 2 * lns[0] + h + 1)
                    act.activation(scr_b[:, h * HB * D:(h + 1) * HB * D],
                                   scr_a[:, h * HB * D:(h + 1) * HB * D], ACT.Square).then_inc(squared, 1)
                lns[0] += 1
                root(small["var"][:, :], small["mean"][:, :], ln_var, lns[0], ln_sd, bias=eps_t[:, 0:1])

            act.wait_ge(consts_made, 5)
            evac(BASE["hop1"], 0)
            act.wait_ge(folded, 1)
            act.activation(by_half(cur[:, :])[:, :, :, :], node_psum(4), ACT.Tanh).then_inc(x_ready, 1)
            features(0)
            evac(BASE["ode"], 1)
            act.wait_ge(folded, 2)
            act.activation(by_half(scr_a), node_psum(4), ACT.Tanh).then_inc(tanh_done, 1)
            layernorm_root()
            evac(BASE["decay0"], 2)
            layernorm_root()
            features(1)
            for q in range(2):
                def relu(k, i, q=q):
                    act.wait_ge(decay_used, i * EARLY_RING + (q * NB + k + 3))
                    for c, (o, w) in enumerate(QUART_CHUNKS):
                        act.wait_ge(tri_done, i * (4 * EARLY_RING) + (4 * (q * NB + k) + 2 * c + 1))
                        dst = decay[k % 2].bitcast(I16)[:, o:o + w]
                        act.activation(dst, bank(c, w), ACT.Relu).then_inc(relu_act, 1)
                each_block(act, relu, EARLY_RING)
            act.wait_ge(decay_used, 4 + 2 * NB)
            act.activation(agg_f[:, 0:QUART], bank(4, QUART), ACT.Copy).then_inc(evac_act, 1)
            layernorm_root()

            def first_parts(n, stacks):
                act.wait_ge(cut_act, n)
                for dst, side in stacks:
                    last = act.activation(dst[side, :], part1[side, :], ACT.Copy)
                last.then_inc(stack_act, 1)

            for it in range(2):
                features(2 + it)
                act.wait_ge(parts, it + 1)
                for h in range(2):
                    act.wait_ge(query_half, 2 * it + h + 1)
                    act.activation(full[:, h * HALF:(h + 1) * HALF], bank(4, HALF), ACT.Identity,
                                   bias=tiny["query_shift"][:, :], scale=D ** -0.5).then_inc(query_f32, 1)
                act.wait_ge(query_f32, 2 * it + 2)
                act.activation(part1, full, ACT.Copy).then_inc(cut_act, 1)
                first_parts(2 * it + 1, ((query12, LO), (query13, LO)))
                root(small["structural"][:, :], small["imp"][:, :], struct_sq, it + 1, struct_done)
                root(small["norm"][:, :], small["rnorm"][:, :], norm_sq, it + 1, norm_rt)
                evac(BASE[f"att{it}"], 4 + 3 * it)
                act.wait_ge(dup_psum, it + 1)
                act.wait_ge(cut_ready, 2 * it + 1)
                act.activation(two(part1), halves_psum(), ACT.Copy).then_inc(cut_act, 1)
                first_parts(2 * it + 2, ((right12, LO), (right21, HI), (right31, HI)))

                def exps(k, i, g):
                    act.wait_ge(negmax_ready, i * RING + (g * NB + k + 1))
                    act.activation(prod[k % 2][:, 0:N], prod[k % 2][:, 0:N], ACT.Exp, bias=negmax[:, k % 2:k % 2 + 1],
                                   accum_out=rowsum[:, k % 2:k % 2 + 1]).then_inc(exp_done, 1)
                each_block(act, lambda k, i: exps(k, i, 2 * it))

                def node_exp(r):
                    act.wait_ge(soft_bias, r + 1)
                    act.activation(small["node_e"][:, :], small["node_z"][:, :], ACT.Exp, bias=tiny["ngmax"][:, :],
                                   accum_out=tiny["psum_"][:, :]).then_inc(part_sum, 1)
                def take(dst, h, first, n):
                    act.wait_ge(turned, 8 * it + n)
                    act.activation(dst[:, h * HALF:(h + 1) * HALF], ps[:, first * BANK:(first + 2) * BANK].bitcast(BF16)
                                   [:, 0:HALF], ACT.Copy).then_inc(turned_act, 1)
                take(right21, 0, 4, 3)
                take(right21, 1, 0, 4)
                take(right31, 0, 2, 5)
                node_exp(2 * it)
                take(right31, 1, 4, 6)
                for h in range(2):
                    act.wait_ge(mask_psum, 2 * it + h + 1)
                    act.activation(mask_row[:, h * HALF:(h + 1) * HALF], bank(4 - 4 * h, HALF), ACT.Copy)\
                        .then_inc(mask_ready, 1)

                def exp_and_sign(k, i):
                    g = 2 * it + 1
                    exps(k, i, g)
                    act.wait_ge(row_cut, i * RING + (it * NB + k + 1))
                    at = i * (RING * NP) + k * NP
                    act.activation(signs[:, bass.ds(at, N)], prod[k % 2][:, 0:N], ACT.Sign,
                                   bias=cut[:, k % 2:k % 2 + 1], scale=-1.0).then_inc(product_free, 1)
                act.wait_ge(turned, 8 * it + 8)
                act.wait_ge(right_ready, 2 * it + 2)
                each_block(act, exp_and_sign)
                node_exp(2 * it + 1)
                root(small["dv"][:, :], small["node_z"][:, :], deg_sq, it + 1, deg_rt)
                evac(BASE[f"up{it}"], 5 + 3 * it)

                act.wait_ge(down_ready, it + 1)

                def columns(k, i):
                    act.wait_ge(signs_t, i * (4 * RING) + (4 * (it * NB + k) + 4))
                    at = i * (RING * P) + k * P
                    dst = sign_cols[k % 2].rearrange("p (b n) -> p b n", b=NB)
                    act.activation(dst, signs3[:, :, bass.ds(at, P)], ACT.Copy).then_inc(col_ready, 1)
                each_block(act, columns)
                evac(BASE[f"up{it}"] + NB, 6 + 3 * it)
                if it == 1:
                    layernorm_root()

        @block.vector
        def _(dve):
            links = [0]

            def link(ins):
                links[0] += 1
                ins.then_inc(dve_chain, 1)
                dve.wait_ge(dve_chain, links[0])

            def evac(n_done, cols=HALF - 2 * BANK):
                dve.wait_ge(block_done, EARLY_RING + n_done)
                dve.tensor_copy(agg_f[:, 2 * BANK:HALF], ps[:, 2 * BANK:HALF]).then_inc(evac_dve, 1)

            def features(r):
                dve.wait_ge(xt_psum, r + 1)
                dve.tensor_copy(xt[:, 2 * BANK:HALF], ps[:, 2 * BANK:HALF]).then_inc(xt_dve, 1)

            lns = [0]

            def layernorm():
                s, q = blocks3(scr_a), blocks3(scr_b)
                mean = small["mean"]
                link(dve.tensor_reduce(mean[:, :], s, axis=X, op=ALU.add))
                link(dve.tensor_scalar(mean[:, :], mean[:, :], 1.0 / D, None, ALU.mult))
                for h in range(2):
                    b = slice(h * HB, (h + 1) * HB)
                    dve.tensor_tensor(s[:, b], s[:, b], per_node(mean[:, :])[:, b], ALU.subtract).then_inc(centred, 1)
                for h in range(2):
                    b = slice(h * HB, (h + 1) * HB)
                    dve.wait_ge(squared, 2 * lns[0] + h + 1)
                    last = dve.tensor_reduce(mean[:, b], q[:, b], axis=X, op=ALU.add)
                link(last)
                dve.tensor_scalar(mean[:, :], mean[:, :], 1.0 / D, None, ALU.mult).then_inc(ln_var, 1)
                lns[0] += 1
                dve.wait_ge(ln_sd, lns[0])
                link(dve.reciprocal(small["var"][:, :], small["var"][:, :]))
                return dve.tensor_tensor(blocks3(cur[:, :]), s, per_node(small["var"][:, :]), ALU.mult)

            dve.wait_ge(const_loaded, 8 * 16)
            dve.tensor_copy(ident_b[:, :], ident).then_inc(consts_cast, 1)
            dve.tensor_copy(tri, full[:, 0:P]).then_inc(consts_cast, 1)
            dve.tensor_copy(rest_tri, full[:, P:2 * P]).then_inc(consts_cast, 1)

            evac(BASE["hop1"])
            features(0)
            evac(BASE["ode"])
            dve.wait_ge(tanh_done, 1)
            link(dve.tensor_tensor(scr_a, scr_a, xw[:, :], ALU.add))
            layernorm().then_inc(x_ready, 1)

            dve.wait_ge(x_ready, 2)
            link(dve.tensor_scalar(scr_a, cur[:, :], -0.1, 1.0, ALU.mult, ALU.add))
            link(dve.tensor_tensor(scr_a, scr_a, cur[:, :], ALU.add))
            evac(BASE["decay0"])
            dve.wait_ge(folded, 3)
            link(dve.tensor_tensor(by_half(scr_b), node_psum(4), by_half(cur[:, :]), ALU.mult))
            link(dve.tensor_reduce(small["mean"][:, :], blocks3(scr_b), axis=X, op=ALU.add))
            link(dve.tensor_scalar(small["mean"][:, :], small["mean"][:, :], 0.01, None, ALU.mult))
            link(dve.tensor_tensor(blocks3(scr_a), blocks3(scr_a), per_node(small["mean"][:, :]), ALU.subtract))
            layernorm().then_inc(x_ready, 1)

            def mask_of(k, i, q):
                slot = landed(dve, f"decay{q}", k, i)
                dve.wait_ge(decay_used, i * EARLY_RING + (q * NB + k + 1))
                dve.tensor_scalar(nbr[(2 * q + k) % 4], slot[:, 0:2 * QUART], 0.0, None, ALU.not_equal)\
                    .then_inc(block_done, 1)

            features(1)
            mask_of(0, 0, 0)
            mask_of(1, 0, 0)
            dve.wait_ge(support_psum, 1)
            sup = support3.rearrange("p (b c d) -> p b c d", c=3, d=D)
            link(dve.tensor_scalar(by_half(scr_a), node_psum(4), float(1 << DECAY_SHIFT), None, ALU.mult))
            link(dve.tensor_copy(sup[:, :, 0], blocks3(scr_a)))
            link(dve.tensor_tensor(blocks3(scr_a), blocks3(scr_a), sup[:, :, 0], ALU.subtract))
            link(dve.tensor_copy(sup[:, :, 1], blocks3(scr_a)))
            dve.tensor_tensor(sup[:, :, 2], blocks3(scr_a), sup[:, :, 1], ALU.subtract).then_inc(support_ready, 1)

            for q in range(2):
                def relu(k, i, q=q):
                    for c, (o, w) in enumerate(QUART_CHUNKS):
                        dve.wait_ge(tri_done, i * (4 * EARLY_RING) + (4 * (q * NB + k) + 2 * c + 2))
                        dst = decay[k % 2].bitcast(I16)[:, QUART + o:QUART + o + w]
                        dve.tensor_scalar(dst, bank(2 + c, w), 0.0, None, ALU.max).then_inc(relu_dve, 1)

                if q:
                    mask_of(0, 0, q)
                    mask_of(1, 0, q)
                with dve.Fori(0, NB // EARLY_RING) as i:
                    for k in range(EARLY_RING):
                        dve.wait_ge(decay_used, i * EARLY_RING + (q * NB + k + 3))
                        relu(k, i)
                        mask_of(k + 2, i, q)
                for k in (NB - 2, NB - 1):
                    dve.wait_ge(decay_used, q * NB + k + 3)
                    relu(k, 0)
            dve.wait_ge(decay_used, 4 + 2 * NB)
            dve.tensor_copy(agg_f[:, QUART:HALF], bank(6, QUART)).then_inc(evac_dve, 1)
            dve.wait_ge(folded, 4)
            dve.wait_ge(biased, 1)
            link(dve.tensor_tensor(by_half(scr_a), node_psum(0), by_half(scr_b), ALU.add))
            link(layernorm())
            dve.tensor_scalar(cur[:, (NB - 1) * D:NB * D], cur[:, (NB - 1) * D:NB * D], real[:, NB - 1:NB], None,
                              ALU.mult).then_inc(x_ready, 1)

            def cut_parts(source, as_halves, stacks, n):
                dve.wait_ge(cut_act, n)
                shape = two if as_halves else (lambda t: t)
                link(dve.tensor_tensor(shape(rest), source, shape(part1), ALU.subtract))
                link(dve.tensor_copy(part2, rest))
                link(dve.tensor_tensor(part3, rest, part2, ALU.subtract))
                dve.wait_ge(stack_act, n)
                for dst, side, src in stacks:
                    last = dve.tensor_copy(dst[side, :], src[side, :])
                last.then_inc(cut_ready, 1)

            def product_piece(name, k, i, c):
                g, steps = PRODUCTS.index(name), steps_of(name)
                if c == 0:
                    landed(dve, name, k, i * (steps // RING))
                    dve.wait_ge(product_free, i * steps + (g * NB + k + 1))
                    if name.startswith("cos") and k >= 2:
                        dve.wait_ge(pruned, i * steps + ((g - 1) * NB + k - 1))
                o, w = PIECES[c]
                w = min(w, N - o)
                dve.wait_ge(piece_ready, i * (4 * steps) + ((g * NB + k) * 4 + c + 1))
                dve.memset(gates[:, 4 * (k % 2) + c:4 * (k % 2) + c + 1], 0.0)
                dve.tensor_tensor_reduce(out=prod[k % 2][:, o:o + w], in0=bank(2 * piece_place(name, k, c)[0], w),
                                         in1=slot_of(name, k)[:, o:o + w], scale=1.0, scalar=-3.0e38, op0=ALU.mult,
                                         op1=ALU.max, accum_out=max4[:, 4 * (k % 2) + c:4 * (k % 2) + c + 1])\
                    .then_inc(piece_read, 1)

            def product_max(name, k, i):
                g, steps = PRODUCTS.index(name), steps_of(name)
                dve.wait_ge(piece_read, i * (4 * steps) + ((g * NB + k) * 4 + 4 + 5))
                one = slice(k % 2, k % 2 + 1)
                dve.tensor_reduce(negmax[:, one], max4[:, 4 * (k % 2):4 * (k % 2) + 4], axis=X, op=ALU.max, negate=True)\
                    .then_inc(negmax_ready, 1)
                if name.startswith("att"):
                    dve.memset(gates[:, 8 + k % 2:9 + k % 2], 0.0).then_inc(block_done, 1)

            def product_pass(name, scale, finish=None):
                for c in range(4):
                    product_piece(name, 0, 0, c)
                product_max(name, 0, 0)

                def block(k, i):
                    product_piece(name, k, i, 0)
                    if finish is not None:
                        scale(k - 1, i)
                    product_piece(name, k, i, 1)
                    if finish is None:
                        scale(k - 1, i)
                    product_piece(name, k, i, 2)
                    product_piece(name, k, i, 3)
                    product_max(name, k, i)
                    if finish is not None:
                        finish(k - 1, i)
                block(1, 0)
                steps = steps_of(name)
                with dve.Fori(0, NB // steps) as i:
                    for k in range(2, 2 + steps):
                        block(k, i)
                scale(NB - 1, 0)
                if finish is not None:
                    finish(NB - 1, 0)

            def column_rows(g):
                dve.wait_ge(colsum_psum, g + 1)
                dve.tensor_copy(col_rows, ps[:, 6 * BANK:8 * BANK]).then_inc(colsum_sbuf, 1)

            def column_sums(g, dst):
                dve.wait_ge(colsum_t, g + 1)
                for h, rows_, cols, at in ((0, (0, 4), 3, 0), (1, (0, 2), 3, 12), (1, (2, 4), 4, 18)):
                    v = bank(6 + h).rearrange("p (s r z) -> p r s z", r=4, z=32)[:, rows_[0]:rows_[1], 0:cols, 0]
                    o = dst[:, at:at + (rows_[1] - rows_[0]) * cols].rearrange("p (r s) -> p r s", s=cols)
                    last = dve.tensor_copy(o, v)
                return last

            def node_softmax(r, threshold, dst):
                dve.tensor_reduce(tiny["pmax"][:, :], small["node_z"][:, :], axis=X, op=ALU.max).then_inc(part_max, 1)
                dve.wait_ge(all_max, r + 1)
                dve.tensor_scalar(tiny["ngmax"][:, :], tiny["gmax"][:, :], -1.0, None, ALU.mult).then_inc(soft_bias, 1)
                dve.wait_ge(all_sum, r + 1)
                link(dve.tensor_scalar(tiny["thr"][:, :], tiny["gsum"][:, :], threshold, None, ALU.mult))
                link(dve.tensor_scalar(dst, small["node_e"][:, :], tiny["thr"][:, :], None, ALU.is_ge))

            for it in range(2):
                th_comp, th_edge, th_node = thresholds(it)
                S = {n: t[:, :] for n, t in small.items()}
                features(2 + it)
                dve.tensor_scalar(tiny["query_shift"][:, :], query_bias, D ** -0.5, None, ALU.mult).then_inc(parts, 1)
                dve.wait_ge(value_psum, it + 1)
                dve.tensor_tensor(by_half(scr_a), node_psum(0), per_feature4(value_bias), ALU.add).then_inc(value_ready, 1)
                dve.wait_ge(proj_psum, it + 1)
                dve.tensor_copy(by_half(xw[:, :]), node_psum(4)).then_inc(proj_read, 1)
                dve.wait_ge(proj_read, it + 1)
                link(dve.tensor_tensor(scr_b, xw[:, :], xw[:, :], ALU.mult))
                link(dve.tensor_reduce(S["imp"], blocks3(scr_b), axis=X, op=ALU.add))
                dve.tensor_scalar(S["imp"], S["imp"], 1e-16, None, ALU.max).then_inc(struct_sq, 1)
                link(dve.tensor_tensor(scr_b, cur[:, :], cur[:, :], ALU.mult))
                link(dve.tensor_reduce(S["rnorm"], blocks3(scr_b), axis=X, op=ALU.add))
                dve.tensor_scalar(S["rnorm"], S["rnorm"], 1e-16, None, ALU.max).then_inc(norm_sq, 1)
                cut_parts(full, False, ((query12, HI, part2), (query13, HI, part3)), 2 * it + 1)
                dve.wait_ge(norm_rt, it + 1)
                link(dve.tensor_scalar(S["rnorm"], S["norm"], 1e-8, None, ALU.max))
                link(dve.reciprocal(S["rnorm"], S["rnorm"]))
                evac(BASE[f"att{it}"])
                dve.wait_ge(dup_psum, it + 1)
                cut_parts(halves_psum(), True, ((right12, HI, part2), (right21, LO, part2), (right31, LO, part3)),
                          2 * it + 2)

                def weigh(k, i, steps=steps_of(f"att{it}")):
                    dve.wait_ge(exp_done, i * steps + (2 * it * NB + k + 1))
                    dve.reciprocal(row_rz[:, k % 2:k % 2 + 1], rowsum[:, k % 2:k % 2 + 1]).then_inc(rz_done, 1)
                    dve.wait_ge(rz_done, i * steps + (it * NB + k + 1))
                    dve.tensor_scalar(rz32[:, k % 2 * 32:(k % 2 + 1) * 32], ones32[:, :], row_rz[:, k % 2:k % 2 + 1],
                                      real[:, bass.ds(i * steps + k, 1)], ALU.mult, ALU.mult).then_inc(rz_ready, 1)
                product_pass(f"att{it}", weigh)
                def take(dst, h, first, n):
                    dve.wait_ge(turned, 8 * it + n)
                    dve.tensor_copy(dst[:, h * HALF:(h + 1) * HALF],
                                    ps[:, first * BANK:(first + 2) * BANK].bitcast(BF16)[:, 0:HALF]).then_inc(turned_dve, 1)
                take(right12, 0, 0, 1)
                take(right12, 1, 2, 2)
                column_rows(2 * it)
                link(column_sums(2 * it, S["colsum"]))
                dve.wait_ge(struct_done, it + 1)
                link(dve.tensor_scalar(S["imp"], S["structural"], 0.5, None, ALU.mult))
                link(dve.scalar_tensor_tensor(out=S["imp"], in0=S["colsum"], scalar=0.5 / N, in1=S["imp"],
                                              op0=ALU.mult, op1=ALU.add))
                link(dve.tensor_tensor(S["imp"], S["imp"], real, ALU.mult))
                link(dve.tensor_tensor(S["node_z"], S["imp"], not_real, ALU.add))
                node_softmax(2 * it, th_comp, S["comp"])
                link(dve.tensor_scalar(S["blocked"], S["comp"], -HUGE, HUGE, ALU.mult, ALU.add))
                for h in range(2):
                    nodes_ = diagonals[:, h * HALF:(h + 1) * HALF].rearrange("p (b n) -> p b n", n=P)
                    dve.tensor_tensor(nodes_, ident_b[:, :].unsqueeze(1).to_broadcast([P, HB, P]),
                                      S["comp"][:, h * HB:(h + 1) * HB].unsqueeze(2).to_broadcast([P, HB, P]), ALU.mult)\
                        .then_inc(diagonal_ready, 1)
                if it == 0:
                    dve.wait_ge(kept_read, 1)
                take(cos13, 0, 0, 7)
                take(cos13, 1, 2, 8)
                dve.wait_ge(turned_act, 4 * it + 4)
                dve.wait_ge(turned_dve, 4 * it + 4)
                for h in range(2):
                    dve.wait_ge(mask_ready, 2 * it + h + 1)
                    part = slice(h * HALF, (h + 1) * HALF)
                    for stack in (right12, right21, right31):
                        last = dve.tensor_tensor(stack[:, part], stack[:, part], mask_row[:, part], ALU.mult)
                    last.then_inc(right_ready, 1)

                def cut_of(k, i):
                    dve.wait_ge(exp_done, i * RING + ((2 * it + 1) * NB + k + 1))
                    one = slice(k % 2, k % 2 + 1)
                    at = bass.ds(i * RING + k, 1)
                    dve.scalar_tensor_tensor(out=cut[:, one], in0=rowsum[:, one], scalar=th_edge,
                                             in1=S["blocked"][:, at], op0=ALU.mult, op1=ALU.add).then_inc(row_cut, 1)

                def prune(k, i):
                    one = slice(k % 2, k % 2 + 1)
                    at = bass.ds(i * RING + k, 1)
                    slot = slot_of(f"cos{it}", k)
                    dve.wait_ge(row_cut, i * RING + (it * NB + k + 1))
                    dve.scalar_tensor_tensor(out=slot[:, 0:N], in0=prod[k % 2][:, 0:N], scalar=cut[:, one],
                                             in1=slot[:, 0:N], op0=ALU.is_ge, op1=ALU.mult,
                                             accum_out=S["conn"][:, at]).then_inc(pruned, 1)
                product_pass(f"cos{it}", cut_of, prune)

                link(dve.memset(signs3[:, :, N:NP], 0))
                link(dve.tensor_tensor(S["imp"], S["conn"], S["norm"], ALU.mult))
                link(dve.tensor_tensor(S["imp"], S["imp"], real, ALU.mult))
                link(dve.tensor_tensor(S["node_z"], S["imp"], not_real, ALU.add))
                node_softmax(2 * it + 1, th_node, S["imp"])
                link(dve.scalar_tensor_tensor(out=S["imp"], in0=S["conn"], scalar=0.0, in1=S["imp"],
                                              op0=ALU.is_gt, op1=ALU.mult))
                link(dve.tensor_tensor(S["imp"], S["imp"], S["comp"], ALU.mult))
                dve.tensor_scalar(S["node_z"], S["conn"], 1e-6, None, ALU.max).then_inc(deg_sq, 1)
                column_rows(2 * it + 1)
                dve.wait_ge(deg_rt, it + 1)
                link(dve.reciprocal(S["dv"], S["dv"]))
                link(dve.tensor_tensor(S["imp"], S["imp"], S["dv"], ALU.mult))
                dve.tensor_tensor(blocks3(cur[:, :]), blocks3(xw[:, :]), per_node(S["imp"]), ALU.mult)\
                    .then_inc(down_ready, 1)

                def down(k, i):
                    slot = landed(dve, f"down{it}", k, i)
                    at = i * (RING * NP) + k * NP
                    dve.scalar_tensor_tensor(out=slot[:, 0:N], in0=signs[:, bass.ds(at, N)], scalar=0.0,
                                             in1=slot[:, 0:N], op0=ALU.is_le, op1=ALU.mult).then_inc(pruned, 1)
                down(0, 0)
                down(1, 0)
                link(column_sums(2 * it + 1, S["edeg"]))
                link(dve.tensor_scalar(S["edeg"], S["edeg"], 1e-6, None, ALU.max))
                link(dve.reciprocal(S["edeg"], S["edeg"]))
                with dve.Fori(0, NB // RING) as i:
                    for k in range(2, 2 + RING):
                        down(k, i)
                evac(BASE[f"up{it}"])
                dve.wait_ge(folded, 5 + 2 * it)
                dve.tensor_tensor(by_half(cur[:, :]), node_psum(4), per_node4(S["edeg"]), ALU.mult).then_inc(up_ready, 1)

                def up(k, i):
                    slot = landed(dve, f"up{it}", k, i)
                    v = slot[:, :].rearrange("p (h n) -> p h n", h=2)
                    for c, (o, w) in enumerate(HALF_CHUNKS):
                        dve.wait_ge(signs_t, i * (4 * RING) + (4 * (it * NB + k) + c + 9))
                        b = 4 + 2 * (c % 2)
                        s = ps[:, b * BANK:(b + 2) * BANK].rearrange("p (h n) -> p h n", h=2)[:, :, 0:w]
                        dve.scalar_tensor_tensor(out=v[:, :, o:o + w], in0=s, scalar=0.0, in1=v[:, :, o:o + w],
                                                 op0=ALU.is_le, op1=ALU.mult).then_inc(up_pruned, 1)
                each_block(dve, up)
                evac(BASE[f"up{it}"] + NB)
                dve.wait_ge(folded, 6 + 2 * it)
                for h in range(2):
                    new = dve.scalar_tensor_tensor(out=by_half(cur[:, :] if it == 0 else scr_a)[:, h],
                                                   in0=node_psum(4)[:, h], scalar=0.0, in1=per_node4(S["dv"])[:, h],
                                                   op0=ALU.max, op1=ALU.mult)
                if it == 0:
                    new.then_inc(x_ready, 1)
                else:
                    link(new)
                    dve.wait_ge(kept, 32)
                    link(dve.tensor_tensor(scr_a, scr_a, xw[:, :], ALU.add))
                    layernorm().then_inc(out_ready, 1)


def kernel(x, adj, L0_gnn_W, L1_gnn_t, L2_gnn_weight, L2_gnn_bias, L3_gnn_W, L3_gnn_Theta, L3_gnn_Wq, L3_gnn_bq,
           L3_gnn_Wv, L3_gnn_bv):
    import concourse.bacc as bacc
    from concourse.bass_utils import run_bass_kernel_spmd

    def f(a):
        return np.asarray(a)

    def nodes(a):
        return np.ascontiguousarray(a.reshape(NB, P, -1).transpose(1, 0, 2).reshape(P, -1))

    x, adj = f(x), f(adj)
    xp = np.zeros((NP, D), np.float32)
    xp[:N] = x
    ap = np.zeros((NP, NP), np.float32)
    ap[:N, :N] = adj
    x_feat = np.ascontiguousarray(xp.T.reshape(D, 2, HALF).transpose(1, 0, 2).reshape(P, HALF))
    w0 = f(L0_gnn_W)

    def twice_diagonal(m):
        t = np.zeros((P, P), np.float32)
        t[:D, :D] = t[D:, D:] = m
        return t
    early = np.concatenate([twice_diagonal(m) for m in
                            (w0[0, :D], w0[0, D:], w0[1, :D], w0[1, D:], f(L2_gnn_weight))], 1)
    late = np.concatenate([twice_diagonal(m) for m in (f(L3_gnn_W), f(L3_gnn_Theta), f(L3_gnn_Wv))]
                          + [np.tile(f(L3_gnn_Wq), (2, 2))], 1)
    rows = np.concatenate([np.broadcast_to(f(b)[None], (P, D)) for b in (L2_gnn_bias, L3_gnn_bv)], 1)
    bq = np.concatenate([f(L3_gnn_bq)] * 2)[:, None]
    eye = np.eye(P, dtype=np.float32)
    twice = np.tile(np.eye(D, dtype=np.float32), (2, 2))
    real = np.ones((P, NB), np.float32)
    real[N - (NB - 1) * P:, NB - 1] = 0
    consts = np.concatenate([eye, twice, real, np.where(real > 0, 0, -HUGE).astype(np.float32)], 1)
    later = np.tri(P, P, -1, dtype=np.float32)
    tri = -P * later + MARK * eye
    decay_consts = np.concatenate([tri, -P - tri], 1)

    arrays = {"adj": ap, "adj_t": np.ascontiguousarray(ap.T), "x_nodes": nodes(xp), "x_feat": x_feat,
              "early_weights": early, "late_weights": late, "rows": rows, "bq": bq, "consts": consts, "decay_consts": decay_consts}
    arrays = {n: np.ascontiguousarray(a) for n, a in arrays.items()}
    nc = bacc.Bacc("TRN2", target_bir_lowering=False, num_devices=1)
    args = [nc.dram_tensor(n, a.shape, F32, kind="ExternalInput").ap() for n, a in arrays.items()]
    kept = nc.dram_tensor("x_kept", (P, NB * D), F32, kind="Internal").ap()
    out = nc.dram_tensor("out", (P, NB, D), F32, kind="ExternalOutput").ap()
    build_program(nc, *args, kept, out)
    r = run_bass_kernel_spmd(nc, [arrays], core_ids=[0])
    got = r.results[0]["out"]
    return np.ascontiguousarray(got.transpose(1, 0, 2).reshape(NP, D)[:N])
```
